# Optimizing a Trainium2 kernel written in Bass

```python
import numpy as np
import jax
import jax.numpy as jnp

def _softmax(x, axis=-1):
    return jax.nn.softmax(x, axis=axis)

def _gelu(x):
    return jax.nn.gelu(x, approximate=True)

def _silu(x):
    return jax.nn.silu(x)

def _sigmoid(x):
    return jax.nn.sigmoid(x)

def _layernorm(x, axis=-1, eps=1e-05):
    m = jnp.mean(x, axis=axis, keepdims=True)
    v = jnp.var(x, axis=axis, keepdims=True)
    return (x - m) / jnp.sqrt(v + eps)

def _scatter_add(tgt, idx, src, axis=0):
    return tgt.at[idx].add(src)

def _segment_sum(src, seg, n):
    return jax.ops.segment_sum(src, seg, n)
kernel_name = 'mk_xattn_seq_d4_seqx_r8_9e0278'

def setup_inputs(seed: int=0):
    np.random.seed(seed)
    _w = jnp.asarray

    def _rec_inputs():
        import jax
        import jax.numpy as jnp
        _rk = jax.random.key(seed)
        x = -0.0002928 + 1 * jax.random.normal(jax.random.fold_in(_rk, 1), (4, 512, 128), jnp.float32)
        _lenS = 512 - jax.random.randint(jax.random.fold_in(_rk, 7), (4,), 0, max(1, 512 // 4) + 1, jnp.int32)
        _lenS2 = 154 - jax.random.randint(jax.random.fold_in(_rk, 8), (4,), 0, max(1, 154 // 4) + 1, jnp.int32)
        _ctx_1024P = jax.random.normal(jax.random.fold_in(_rk, 11), (4, 16, 128), jnp.float32)
        _ctx_1024c = jax.random.dirichlet(jax.random.fold_in(_rk, 511), 0.3 * jnp.ones((16,), jnp.float32), (4, 154))
        _ctx_1024t = jnp.einsum('bsk,bkd->bsd', _ctx_1024c, _ctx_1024P)
        _ctx_1024t = _ctx_1024t * jax.lax.rsqrt(jnp.mean(jnp.square(_ctx_1024t)) + 1e-12) * 0.953939
        ctx_1024 = 0.000227908 + 0.99994 * (_ctx_1024t + 0.3 * jax.random.normal(jax.random.fold_in(_rk, 611), (4, 154, 128), jnp.float32))
        return (x, ctx_1024)
    x, ctx_1024 = _rec_inputs()

    def _L0_xattn_setup():
        import jax, jax.numpy as jnp
        import numpy as np
        B, T, S, D, H, F = (2, 256, 64, 128, 16, 512)
        DH = D // H
        EPS = 1e-05

        def _ln(x, g, b):
            m = x.mean(-1, keepdims=True)
            v = ((x - m) ** 2).mean(-1, keepdims=True)
            return (x - m) * jax.lax.rsqrt(v + EPS) * g + b
        key = jax.random.key(seed)
        ks = jax.random.split(key, 8)
        w = lambda k, shape: jax.random.normal(k, shape, dtype=jnp.float32) * 0.02
        return {'x': jax.random.normal(ks[0], (B, T, D), dtype=jnp.float32), 'context': jax.random.normal(ks[1], (B, S, D), dtype=jnp.float32), 'w_qkv': w(ks[2], (D, 3 * D)), 'b_qkv': jnp.zeros((3 * D,), jnp.float32), 'w_ckv': w(ks[3], (D, 2 * D)), 'b_ckv': jnp.zeros((2 * D,), jnp.float32), 'g1': jnp.ones((D,), jnp.float32), 'be1': jnp.zeros((D,), jnp.float32), 'g2': jnp.ones((D,), jnp.float32), 'be2': jnp.zeros((D,), jnp.float32), 'gf': jnp.ones((D,), jnp.float32), 'bf': jnp.zeros((D,), jnp.float32), 'w1': w(ks[4], (D, F)), 'b1': jnp.zeros((F,), jnp.float32), 'w2': w(ks[5], (F, D)), 'b2': jnp.zeros((D,), jnp.float32)}
    _L0_xattn_all = _L0_xattn_setup()
    _L0_xattn_in = {k: v for k, v in _L0_xattn_all.items() if k in ('w_qkv', 'b_qkv', 'w_ckv', 'b_ckv', 'g1', 'be1', 'g2', 'be2', 'gf', 'bf', 'w1', 'b1', 'w2', 'b2')}
    del _L0_xattn_all

    def _L1_xattn_setup():
        import jax, jax.numpy as jnp
        import numpy as np
        from functools import partial
        HEADS = 16
        DIM_HEAD = 64
        SCALE = DIM_HEAD ** (-0.5)
        MAX_ALLOWABLE = 128 * 128 * 8
        EPS = 1e-05

        def ln32(x, scale, bias):
            x32 = x.astype(jnp.float32)
            mean = jnp.mean(x32, axis=-1, keepdims=True)
            var = jnp.mean(jnp.square(x32 - mean), axis=-1, keepdims=True)
            y = (x32 - mean) * jax.lax.rsqrt(var + EPS) * scale.astype(jnp.float32) + bias.astype(jnp.float32)
            return y.astype(x.dtype)

        def heads_to_batch(t):
            b, s, d = t.shape
            return t.reshape(b, s, HEADS, d // HEADS).transpose(0, 2, 1, 3).reshape(b * HEADS, s, d // HEADS)

        def batch_to_heads(t):
            bh, s, dh = t.shape
            return t.reshape(bh // HEADS, HEADS, s, dh).transpose(0, 2, 1, 3).reshape(bh // HEADS, s, dh * HEADS)

        def _max_pow2(n):
            i = 1
            while n % 2 == 0:
                i *= 2
                n //= 2
            return i

        def sdpa(q, k, v):
            scores = jnp.einsum('bid,bjd->bij', q, k) * SCALE
            probs = jax.nn.softmax(scores, axis=2)
            return jnp.einsum('bij,bjd->bid', probs, v)

        def lowmem_attention(q, k, v):
            dimprod = q.shape[0] * q.shape[1] * k.shape[1]
            true_divisor = dimprod / MAX_ALLOWABLE
            if true_divisor < 1:
                n_splits = 1
            elif true_divisor >= q.shape[0]:
                n_splits = q.shape[0]
            else:
                nearest_pow2 = 2 ** np.round(np.log2(true_divisor))
                n_splits = int(min(_max_pow2(q.shape[0]), nearest_pow2))
            nq, nk, nv = [h.reshape(n_splits, h.shape[0] // n_splits, h.shape[-2], h.shape[-1]) for h in (q, k, v)]
            outs = jax.lax.scan(lambda c, a: (None, sdpa(*a)), None, (nq, nk, nv))[1]
            return outs.reshape(-1, outs.shape[-2], outs.shape[-1])

        def attention(x, ctx, Wq, Wkv, Wo, bo):
            q = x @ Wq
            k, v = jnp.split(ctx @ Wkv, 2, axis=-1)
            out = lowmem_attention(heads_to_batch(q), heads_to_batch(k), heads_to_batch(v))
            return batch_to_heads(out) @ Wo + bo

        def geglu_ff(x, Wff1, bff1, Wff2, bff2):
            h = x @ Wff1 + bff1
            lin, gelu = jnp.split(h, 2, axis=-1)
            h = lin * (gelu * jax.nn.sigmoid(1.702 * gelu))
            return h @ Wff2 + bff2
        key = jax.random.key(seed)
        ks = jax.random.split(key, 12)
        B, S, D, CTX = (4, 256, 128, 77)
        s = 0.02
        return {'hidden_states': jax.random.normal(ks[0], (B, S, D), jnp.float32), 'context': jax.random.normal(ks[1], (B, CTX, D), jnp.float32), 'Wq1': jax.random.normal(ks[2], (D, D), jnp.float32) * s, 'Wkv1': jax.random.normal(ks[3], (D, 2 * D), jnp.float32) * s, 'Wo1': jax.random.normal(ks[4], (D, D), jnp.float32) * s, 'bo1': jnp.zeros((D,), jnp.float32), 'Wq2': jax.random.normal(ks[5], (D, D), jnp.float32) * s, 'Wkv2': jax.random.normal(ks[6], (D, 2 * D), jnp.float32) * s, 'Wo2': jax.random.normal(ks[7], (D, D), jnp.float32) * s, 'bo2': jnp.zeros((D,), jnp.float32), 'Wff1': jax.random.normal(ks[8], (D, 8 * D), jnp.float32) * s, 'bff1': jnp.zeros((8 * D,), jnp.float32), 'Wff2': jax.random.normal(ks[9], (4 * D, D), jnp.float32) * s, 'bff2': jnp.zeros((D,), jnp.float32), 'ln1_s': jnp.ones((D,), jnp.float32), 'ln1_b': jnp.zeros((D,), jnp.float32), 'ln2_s': jnp.ones((D,), jnp.float32), 'ln2_b': jnp.zeros((D,), jnp.float32), 'ln3_s': jnp.ones((D,), jnp.float32), 'ln3_b': jnp.zeros((D,), jnp.float32)}
    _L1_xattn_all = _L1_xattn_setup()
    _L1_xattn_in = {k: v for k, v in _L1_xattn_all.items() if k in ('Wq1', 'Wkv1', 'Wo1', 'bo1', 'Wq2', 'Wkv2', 'Wo2', 'bo2', 'Wff1', 'bff1', 'Wff2', 'bff2', 'ln1_s', 'ln1_b', 'ln2_s', 'ln2_b', 'ln3_s', 'ln3_b')}
    del _L1_xattn_all

    def _L2_xattn_setup():
        import jax, jax.numpy as jnp
        import numpy as np
        LN_EPS = 1e-05
        SCALE = 1.0 / 8.0

        def layernorm(x, g, b):
            m = jnp.mean(x, axis=-1, keepdims=True)
            v = jnp.mean(jnp.square(x - m), axis=-1, keepdims=True)
            return (x - m) * jax.lax.rsqrt(v + LN_EPS) * g + b

        def attention_block(q_in, kv_in, wq, bq, wk, bk, wv, bv, g, b):
            Q = q_in @ wq + bq
            K = kv_in @ wk + bk
            V = kv_in @ wv + bv
            scores = jnp.einsum('bsd,btd->bst', Q, K) * SCALE
            A = jax.nn.softmax(scores, axis=-1)
            out = jnp.einsum('bst,btd->bsd', A, V)
            return layernorm(out + q_in, g, b)
        key = jax.random.key(seed)
        ks = jax.random.split(key, 16)
        B, S, T, D = (4, 256, 256, 128)
        w = lambda k: jax.random.normal(k, (D, D), dtype=jnp.float32) * 0.02
        z = jnp.zeros((D,), dtype=jnp.float32)
        o = jnp.ones((D,), dtype=jnp.float32)
        return {'x': jax.random.normal(ks[0], (B, S, D), dtype=jnp.float32), 'y': jax.random.normal(ks[1], (B, T, D), dtype=jnp.float32), 'wq_m': w(ks[2]), 'bq_m': z, 'wk_m': w(ks[3]), 'bk_m': z, 'wv_m': w(ks[4]), 'bv_m': z, 'g_m': o, 'b_m': z, 'wq_c': w(ks[5]), 'bq_c': z, 'wk_c': w(ks[6]), 'bk_c': z, 'wv_c': w(ks[7]), 'bv_c': z, 'g_c': o, 'b_c': z, 'f0_w': w(ks[8]), 'f0_b': z, 'f1_w': w(ks[9]), 'f1_b': z, 'g_d': o, 'b_d': z}
    _L2_xattn_all = _L2_xattn_setup()
    _L2_xattn_in = {k: v for k, v in _L2_xattn_all.items() if k in ('wq_m', 'bq_m', 'wk_m', 'bk_m', 'wv_m', 'bv_m', 'g_m', 'b_m', 'wq_c', 'bq_c', 'wk_c', 'bk_c', 'wv_c', 'bv_c', 'g_c', 'b_c', 'f0_w', 'f0_b', 'f1_w', 'f1_b', 'g_d', 'b_d')}
    del _L2_xattn_all

    def _L3_xattn_setup():
        import jax, jax.numpy as jnp
        import numpy as np
        EMBED = 128
        key = jax.random.key(seed)
        k1, k2, k3, k4, k5 = jax.random.split(key, 5)
        B, Sl, Sr, D = (4, 512, 512, EMBED)
        left = jax.random.normal(k1, (B, Sl, D), dtype=jnp.float32)
        right = jax.random.normal(k2, (B, Sr, D), dtype=jnp.float32)
        scale = 1.0 / np.sqrt(D)
        Wq = jax.random.normal(k3, (D, D), dtype=jnp.float32) * scale
        Wk = jax.random.normal(k4, (D, D), dtype=jnp.float32) * scale
        Wv = jax.random.normal(k5, (D, D), dtype=jnp.float32) * scale
        return {'left': left, 'right': right, 'Wq': Wq, 'Wk': Wk, 'Wv': Wv}
    _L3_xattn_all = _L3_xattn_setup()
    _L3_xattn_in = {k: v for k, v in _L3_xattn_all.items() if k in ('Wq', 'Wk', 'Wv')}
    del _L3_xattn_all
    return {'x': x, 'ctx_1024': ctx_1024, 'L0_xattn_w_qkv': _L0_xattn_in['w_qkv'], 'L0_xattn_b_qkv': _L0_xattn_in['b_qkv'], 'L0_xattn_w_ckv': _L0_xattn_in['w_ckv'], 'L0_xattn_b_ckv': _L0_xattn_in['b_ckv'], 'L0_xattn_g1': _L0_xattn_in['g1'], 'L0_xattn_be1': _L0_xattn_in['be1'], 'L0_xattn_g2': _L0_xattn_in['g2'], 'L0_xattn_be2': _L0_xattn_in['be2'], 'L0_xattn_gf': _L0_xattn_in['gf'], 'L0_xattn_bf': _L0_xattn_in['bf'], 'L0_xattn_w1': _L0_xattn_in['w1'], 'L0_xattn_b1': _L0_xattn_in['b1'], 'L0_xattn_w2': _L0_xattn_in['w2'], 'L0_xattn_b2': _L0_xattn_in['b2'], 'L1_xattn_Wq1': _L1_xattn_in['Wq1'], 'L1_xattn_Wkv1': _L1_xattn_in['Wkv1'], 'L1_xattn_Wo1': _L1_xattn_in['Wo1'], 'L1_xattn_bo1': _L1_xattn_in['bo1'], 'L1_xattn_Wq2': _L1_xattn_in['Wq2'], 'L1_xattn_Wkv2': _L1_xattn_in['Wkv2'], 'L1_xattn_Wo2': _L1_xattn_in['Wo2'], 'L1_xattn_bo2': _L1_xattn_in['bo2'], 'L1_xattn_Wff1': _L1_xattn_in['Wff1'], 'L1_xattn_bff1': _L1_xattn_in['bff1'], 'L1_xattn_Wff2': _L1_xattn_in['Wff2'], 'L1_xattn_bff2': _L1_xattn_in['bff2'], 'L1_xattn_ln1_s': _L1_xattn_in['ln1_s'], 'L1_xattn_ln1_b': _L1_xattn_in['ln1_b'], 'L1_xattn_ln2_s': _L1_xattn_in['ln2_s'], 'L1_xattn_ln2_b': _L1_xattn_in['ln2_b'], 'L1_xattn_ln3_s': _L1_xattn_in['ln3_s'], 'L1_xattn_ln3_b': _L1_xattn_in['ln3_b'], 'L2_xattn_wq_m': _L2_xattn_in['wq_m'], 'L2_xattn_bq_m': _L2_xattn_in['bq_m'], 'L2_xattn_wk_m': _L2_xattn_in['wk_m'], 'L2_xattn_bk_m': _L2_xattn_in['bk_m'], 'L2_xattn_wv_m': _L2_xattn_in['wv_m'], 'L2_xattn_bv_m': _L2_xattn_in['bv_m'], 'L2_xattn_g_m': _L2_xattn_in['g_m'], 'L2_xattn_b_m': _L2_xattn_in['b_m'], 'L2_xattn_wq_c': _L2_xattn_in['wq_c'], 'L2_xattn_bq_c': _L2_xattn_in['bq_c'], 'L2_xattn_wk_c': _L2_xattn_in['wk_c'], 'L2_xattn_bk_c': _L2_xattn_in['bk_c'], 'L2_xattn_wv_c': _L2_xattn_in['wv_c'], 'L2_xattn_bv_c': _L2_xattn_in['bv_c'], 'L2_xattn_g_c': _L2_xattn_in['g_c'], 'L2_xattn_b_c': _L2_xattn_in['b_c'], 'L2_xattn_f0_w': _L2_xattn_in['f0_w'], 'L2_xattn_f0_b': _L2_xattn_in['f0_b'], 'L2_xattn_f1_w': _L2_xattn_in['f1_w'], 'L2_xattn_f1_b': _L2_xattn_in['f1_b'], 'L2_xattn_g_d': _L2_xattn_in['g_d'], 'L2_xattn_b_d': _L2_xattn_in['b_d'], 'L3_xattn_Wq': _L3_xattn_in['Wq'], 'L3_xattn_Wk': _L3_xattn_in['Wk'], 'L3_xattn_Wv': _L3_xattn_in['Wv']}

def reference(x, ctx_1024, L0_xattn_w_qkv, L0_xattn_b_qkv, L0_xattn_w_ckv, L0_xattn_b_ckv, L0_xattn_g1, L0_xattn_be1, L0_xattn_g2, L0_xattn_be2, L0_xattn_gf, L0_xattn_bf, L0_xattn_w1, L0_xattn_b1, L0_xattn_w2, L0_xattn_b2, L1_xattn_Wq1, L1_xattn_Wkv1, L1_xattn_Wo1, L1_xattn_bo1, L1_xattn_Wq2, L1_xattn_Wkv2, L1_xattn_Wo2, L1_xattn_bo2, L1_xattn_Wff1, L1_xattn_bff1, L1_xattn_Wff2, L1_xattn_bff2, L1_xattn_ln1_s, L1_xattn_ln1_b, L1_xattn_ln2_s, L1_xattn_ln2_b, L1_xattn_ln3_s, L1_xattn_ln3_b, L2_xattn_wq_m, L2_xattn_bq_m, L2_xattn_wk_m, L2_xattn_bk_m, L2_xattn_wv_m, L2_xattn_bv_m, L2_xattn_g_m, L2_xattn_b_m, L2_xattn_wq_c, L2_xattn_bq_c, L2_xattn_wk_c, L2_xattn_bk_c, L2_xattn_wv_c, L2_xattn_bv_c, L2_xattn_g_c, L2_xattn_b_c, L2_xattn_f0_w, L2_xattn_f0_b, L2_xattn_f1_w, L2_xattn_f1_b, L2_xattn_g_d, L2_xattn_b_d, L3_xattn_Wq, L3_xattn_Wk, L3_xattn_Wv):
    import jax
    import jax.numpy as jnp

    def _L0_xattn_ref(x, context, w_qkv, b_qkv, w_ckv, b_ckv, g1, be1, g2, be2, gf, bf, w1, b1, w2, b2):
        import jax, jax.numpy as jnp
        import numpy as np
        B, T, S, D, H, F = (2, 256, 64, 128, 16, 512)
        DH = D // H
        EPS = 1e-05

        def _ln(x, g, b):
            m = x.mean(-1, keepdims=True)
            v = ((x - m) ** 2).mean(-1, keepdims=True)
            return (x - m) * jax.lax.rsqrt(v + EPS) * g + b
        b, t, d = x.shape
        s = context.shape[1]
        h, dh = (H, d // H)
        qkv = (_ln(x, g1, be1) @ w_qkv + b_qkv).reshape(b, t, 3, h, dh)
        q, k_self, v_self = (qkv[:, :, 0], qkv[:, :, 1], qkv[:, :, 2])
        ckv = (context @ w_ckv + b_ckv).reshape(b, s, 2, h, dh)
        k_ctx, v_ctx = (ckv[:, :, 0], ckv[:, :, 1])
        k = jnp.concatenate([k_self, k_ctx], axis=1)
        v = jnp.concatenate([v_self, v_ctx], axis=1)
        scale = 1.0 / jnp.sqrt(jnp.float32(dh))
        scores = jnp.einsum('bthd,bshd->bhts', q, k) * scale
        i = jnp.arange(t)[:, None]
        j = jnp.arange(t + s)[None, :]
        mask = (j >= t) | (j <= i)
        scores = jnp.where(mask, scores, -jnp.inf)
        attn = jax.nn.softmax(scores, axis=-1)
        attn_out = jnp.einsum('bhts,bshd->bthd', attn, v).reshape(b, t, d)
        x = x + attn_out
        hdn = _ln(_ln(x, g2, be2), gf, bf) @ w1 + b1
        hdn = jax.nn.gelu(hdn, approximate=False)
        x = x + (hdn @ w2 + b2)
        return x

    def _L1_xattn_ref(hidden_states, context, Wq1, Wkv1, Wo1, bo1, Wq2, Wkv2, Wo2, bo2, Wff1, bff1, Wff2, bff2, ln1_s, ln1_b, ln2_s, ln2_b, ln3_s, ln3_b):
        import jax, jax.numpy as jnp
        import numpy as np
        from functools import partial
        HEADS = 16
        DIM_HEAD = 64
        SCALE = DIM_HEAD ** (-0.5)
        MAX_ALLOWABLE = 128 * 128 * 8
        EPS = 1e-05

        def ln32(x, scale, bias):
            x32 = x.astype(jnp.float32)
            mean = jnp.mean(x32, axis=-1, keepdims=True)
            var = jnp.mean(jnp.square(x32 - mean), axis=-1, keepdims=True)
            y = (x32 - mean) * jax.lax.rsqrt(var + EPS) * scale.astype(jnp.float32) + bias.astype(jnp.float32)
            return y.astype(x.dtype)

        def heads_to_batch(t):
            b, s, d = t.shape
            return t.reshape(b, s, HEADS, d // HEADS).transpose(0, 2, 1, 3).reshape(b * HEADS, s, d // HEADS)

        def batch_to_heads(t):
            bh, s, dh = t.shape
            return t.reshape(bh // HEADS, HEADS, s, dh).transpose(0, 2, 1, 3).reshape(bh // HEADS, s, dh * HEADS)

        def _max_pow2(n):
            i = 1
            while n % 2 == 0:
                i *= 2
                n //= 2
            return i

        def sdpa(q, k, v):
            scores = jnp.einsum('bid,bjd->bij', q, k) * SCALE
            probs = jax.nn.softmax(scores, axis=2)
            return jnp.einsum('bij,bjd->bid', probs, v)

        def lowmem_attention(q, k, v):
            dimprod = q.shape[0] * q.shape[1] * k.shape[1]
            true_divisor = dimprod / MAX_ALLOWABLE
            if true_divisor < 1:
                n_splits = 1
            elif true_divisor >= q.shape[0]:
                n_splits = q.shape[0]
            else:
                nearest_pow2 = 2 ** np.round(np.log2(true_divisor))
                n_splits = int(min(_max_pow2(q.shape[0]), nearest_pow2))
            nq, nk, nv = [h.reshape(n_splits, h.shape[0] // n_splits, h.shape[-2], h.shape[-1]) for h in (q, k, v)]
            outs = jax.lax.scan(lambda c, a: (None, sdpa(*a)), None, (nq, nk, nv))[1]
            return outs.reshape(-1, outs.shape[-2], outs.shape[-1])

        def attention(x, ctx, Wq, Wkv, Wo, bo):
            q = x @ Wq
            k, v = jnp.split(ctx @ Wkv, 2, axis=-1)
            out = lowmem_attention(heads_to_batch(q), heads_to_batch(k), heads_to_batch(v))
            return batch_to_heads(out) @ Wo + bo

        def geglu_ff(x, Wff1, bff1, Wff2, bff2):
            h = x @ Wff1 + bff1
            lin, gelu = jnp.split(h, 2, axis=-1)
            h = lin * (gelu * jax.nn.sigmoid(1.702 * gelu))
            return h @ Wff2 + bff2
        x = hidden_states
        x = attention(ln32(x, ln1_s, ln1_b), ln32(x, ln1_s, ln1_b), Wq1, Wkv1, Wo1, bo1) + x
        x = attention(ln32(x, ln2_s, ln2_b), context, Wq2, Wkv2, Wo2, bo2) + x
        x = geglu_ff(ln32(x, ln3_s, ln3_b), Wff1, bff1, Wff2, bff2) + x
        return x

    def _L2_xattn_ref(x, y, wq_m, bq_m, wk_m, bk_m, wv_m, bv_m, g_m, b_m, wq_c, bq_c, wk_c, bk_c, wv_c, bv_c, g_c, b_c, f0_w, f0_b, f1_w, f1_b, g_d, b_d):
        import jax, jax.numpy as jnp
        import numpy as np
        LN_EPS = 1e-05
        SCALE = 1.0 / 8.0

        def layernorm(x, g, b):
            m = jnp.mean(x, axis=-1, keepdims=True)
            v = jnp.mean(jnp.square(x - m), axis=-1, keepdims=True)
            return (x - m) * jax.lax.rsqrt(v + LN_EPS) * g + b

        def attention_block(q_in, kv_in, wq, bq, wk, bk, wv, bv, g, b):
            Q = q_in @ wq + bq
            K = kv_in @ wk + bk
            V = kv_in @ wv + bv
            scores = jnp.einsum('bsd,btd->bst', Q, K) * SCALE
            A = jax.nn.softmax(scores, axis=-1)
            out = jnp.einsum('bst,btd->bsd', A, V)
            return layernorm(out + q_in, g, b)
        res = x
        x = layernorm(attention_block(x, x, wq_m, bq_m, wk_m, bk_m, wv_m, bv_m, g_m, b_m) + res, g_d, b_d)
        res = x
        x = layernorm(attention_block(x, y, wq_c, bq_c, wk_c, bk_c, wv_c, bv_c, g_c, b_c) + res, g_d, b_d)
        res = x
        x = jax.nn.gelu(x @ f0_w + f0_b, approximate=False)
        x = jax.nn.gelu(x @ f1_w + f1_b, approximate=False)
        return layernorm(x + res, g_d, b_d)

    def _L3_xattn_ref(left, right, Wq, Wk, Wv):
        import jax, jax.numpy as jnp
        import numpy as np
        EMBED = 128
        q = jnp.einsum('bip,pd->bid', left, Wq)
        k = jnp.einsum('bjp,pd->bjd', right, Wk)
        v = jnp.einsum('bjp,pd->bjd', right, Wv)
        d = q.shape[-1]
        scores = jnp.einsum('bip,bjp->bij', q, k) * d ** (-0.5)
        attn = jax.nn.softmax(scores, axis=-1)
        out = jnp.einsum('bis,bsj->bij', attn, v)
        return out + left
    x = _L0_xattn_ref(x, ctx_1024, L0_xattn_w_qkv, L0_xattn_b_qkv, L0_xattn_w_ckv, L0_xattn_b_ckv, L0_xattn_g1, L0_xattn_be1, L0_xattn_g2, L0_xattn_be2, L0_xattn_gf, L0_xattn_bf, L0_xattn_w1, L0_xattn_b1, L0_xattn_w2, L0_xattn_b2)
    x = _L1_xattn_ref(x, ctx_1024, L1_xattn_Wq1, L1_xattn_Wkv1, L1_xattn_Wo1, L1_xattn_bo1, L1_xattn_Wq2, L1_xattn_Wkv2, L1_xattn_Wo2, L1_xattn_bo2, L1_xattn_Wff1, L1_xattn_bff1, L1_xattn_Wff2, L1_xattn_bff2, L1_xattn_ln1_s, L1_xattn_ln1_b, L1_xattn_ln2_s, L1_xattn_ln2_b, L1_xattn_ln3_s, L1_xattn_ln3_b)
    x = _L2_xattn_ref(x, ctx_1024, L2_xattn_wq_m, L2_xattn_bq_m, L2_xattn_wk_m, L2_xattn_bk_m, L2_xattn_wv_m, L2_xattn_bv_m, L2_xattn_g_m, L2_xattn_b_m, L2_xattn_wq_c, L2_xattn_bq_c, L2_xattn_wk_c, L2_xattn_bk_c, L2_xattn_wv_c, L2_xattn_bv_c, L2_xattn_g_c, L2_xattn_b_c, L2_xattn_f0_w, L2_xattn_f0_b, L2_xattn_f1_w, L2_xattn_f1_b, L2_xattn_g_d, L2_xattn_b_d)
    x = _L3_xattn_ref(x, ctx_1024, L3_xattn_Wq, L3_xattn_Wk, L3_xattn_Wv)
    return x

_drawn_inputs = setup_inputs


def setup_inputs(seed=0):
    import zlib

    import numpy as np

    out = dict(_drawn_inputs(seed))
    spreads = {'L0_xattn_b_qkv': (0.0, 0.1),
     'L0_xattn_b_ckv': (0.0, 0.1),
     'L0_xattn_g1': (1.0, 0.6),
     'L0_xattn_be1': (0.0, 0.8),
     'L0_xattn_g2': (1.0, 0.6),
     'L0_xattn_be2': (0.0, 2.0),
     'L0_xattn_gf': (1.0, 0.6),
     'L0_xattn_bf': (0.0, 0.8),
     'L0_xattn_b1': (0.0, 0.363),
     'L0_xattn_b2': (0.0, 0.1),
     'L1_xattn_bo1': (0.0, 0.338),
     'L1_xattn_bo2': (0.0, 0.363),
     'L1_xattn_bff1': (0.0, 0.8),
     'L1_xattn_bff2': (0.0, 0.517),
     'L1_xattn_ln1_s': (1.0, 0.6),
     'L1_xattn_ln1_b': (0.0, 0.8),
     'L1_xattn_ln2_s': (1.0, 0.6),
     'L1_xattn_ln2_b': (0.0, 2.0),
     'L1_xattn_ln3_s': (1.0, 0.6),
     'L1_xattn_ln3_b': (0.0, 0.8),
     'L2_xattn_bq_m': (0.0, 2.0),
     'L2_xattn_bk_m': (0.0, 2.0),
     'L2_xattn_bv_m': (0.0, 2.0),
     'L2_xattn_g_m': (1.0, 0.572),
     'L2_xattn_b_m': (0.0, 0.579),
     'L2_xattn_bq_c': (0.0, 0.8),
     'L2_xattn_bk_c': (0.0, 2.0),
     'L2_xattn_bv_c': (0.0, 0.1),
     'L2_xattn_g_c': (1.0, 0.2),
     'L2_xattn_b_c': (0.0, 0.1),
     'L2_xattn_f0_b': (0.0, 0.8),
     'L2_xattn_f1_b': (0.0, 0.1),
     'L2_xattn_g_d': (1.0, 0.2),
     'L2_xattn_b_d': (0.0, 0.1)}
    factors = {'L0_xattn_w_qkv': 4.887,
     'L1_xattn_Wq1': 8.0,
     'L1_xattn_Wkv1': 7.443,
     'L1_xattn_Wo1': 8.0,
     'L1_xattn_Wq2': 64.0,
     'L1_xattn_Wkv2': 10.976,
     'L1_xattn_Wff1': 4.475,
     'L1_xattn_Wff2': 4.294,
     'L2_xattn_wq_m': 8.0,
     'L2_xattn_wk_m': 8.0,
     'L2_xattn_wv_m': 2.819,
     'L2_xattn_wq_c': 8.0,
     'L2_xattn_wk_c': 8.0,
     'L2_xattn_f0_w': 5.417,
     'L2_xattn_f1_w': 5.022,
     'L1_xattn_Wo2': 3.132}
    for name, (base, spread) in spreads.items():
        noise = np.random.default_rng([zlib.crc32(name.encode()), seed]).standard_normal(out[name].shape)
        drawn = base * np.exp(spread * noise) if base else spread * noise
        out[name] = jnp.asarray(drawn.astype(out[name].dtype))
    for name, factor in factors.items():
        out[name] = (out[name] * factor).astype(out[name].dtype)
    return out
```

```python
from contextlib import ExitStack

import concourse.bass as bass
from concourse import mybir

F32 = mybir.dt.float32
BF16 = mybir.dt.bfloat16
ALU = mybir.AluOpType
ACT = mybir.ActivationFunctionType
AX = mybir.AxisListType

P = 128
B, T, D = 4, 512, 128
S = 154
SB = S - P
NT = T // P
H, DH = 16, 8
PAIRS = H // 2
GROUPS = H // 4
TERMS = 6
KR = TERMS * DH
NEG = 2 * KR
Q_RUNS = ((0, 3, 0, True), (3, 2, 1, True), (5, 1, 2, True))
K_RUNS = ((0, 3, 0, False), (3, 2, 0, False), (5, 1, 0, False))
QR = 6
ONES = 1.0019378662109375
FC = 4
EPS = 1e-5
NORMS = 11
LOWEST = -3.0e38
MASKED = -1.0e30
STACKED = 16 * 2
BOUNCED = 16 * len(Q_RUNS)
NEG_ROWS = 16 * 2

CAUSAL, SELF, CROSS = 0, 1, 2
KEY_TILES = {CAUSAL: (0, 1, 2, 3, "A", "B"), SELF: (0, 1, 2, 3), CROSS: ("A", "B")}
HEAD_SCALE = {CAUSAL: float(DH) ** -0.5, SELF: 0.125, CROSS: 0.125}

FIRST_WEIGHTS = 12

COLUMNS = [
    ("L0_xattn_b_qkv", 3), ("L0_xattn_b_ckv", 2), ("L0_xattn_g1", 1), ("L0_xattn_be1", 1),
    ("L0_xattn_gf", 1), ("L0_xattn_bf", 1), ("L0_xattn_b1", 4),
    ("L1_xattn_ln1_s", 1), ("L1_xattn_ln1_b", 1), ("L1_xattn_ln2_s", 1), ("L1_xattn_ln2_b", 1),
    ("L1_xattn_ln3_s", 1), ("L1_xattn_ln3_b", 1), ("L1_xattn_bff1", 8),
    ("L2_xattn_bq_m", 1), ("L2_xattn_bk_m", 1), ("L2_xattn_bq_c", 1), ("L2_xattn_bk_c", 1),
    ("L2_xattn_f0_b", 1),
]
BROADCASTS = [
    ("L0_xattn_b_qkv", 2 * D), ("L0_xattn_b_ckv", D), ("L0_xattn_g2", 0), ("L0_xattn_be2", 0),
    ("L0_xattn_b2", 0), ("L1_xattn_bo1", 0), ("L1_xattn_bo2", 0), ("L1_xattn_bff2", 0),
    ("L2_xattn_bv_m", 0), ("L2_xattn_g_m", 0), ("L2_xattn_b_m", 0), ("L2_xattn_bv_c", 0),
    ("L2_xattn_g_c", 0), ("L2_xattn_b_c", 0), ("L2_xattn_f1_b", 0), ("L2_xattn_g_d", 0),
    ("L2_xattn_b_d", 0),
]
WEIGHTS = [
    ("L0_xattn_w_ckv", 2 * D), ("L1_xattn_Wkv2", 2 * D), ("L0_xattn_w_qkv", 3 * D),
    ("L0_xattn_w1", 4 * D), ("L0_xattn_w2", 4 * D),
    ("L1_xattn_Wq1", D), ("L1_xattn_Wkv1", 2 * D), ("L1_xattn_Wo1", D), ("L1_xattn_Wq2", D),
    ("L1_xattn_Wo2", D), ("L1_xattn_Wff1", 8 * D), ("L1_xattn_Wff2", 4 * D),
    ("L2_xattn_wk_c", D), ("L2_xattn_wv_c", D), ("L3_xattn_Wk", D), ("L3_xattn_Wv", D),
    ("L2_xattn_wq_m", D), ("L2_xattn_wk_m", D), ("L2_xattn_wv_m", D),
    ("L2_xattn_wq_c", D), ("L2_xattn_f0_w", D), ("L2_xattn_f1_w", D), ("L3_xattn_Wq", D),
]


def four_cross_attention_blocks(nc: bass.Bass, out: bass.AP, **inp: bass.AP):
    with ExitStack() as ctx:
        def sb(name, shape, dt=F32):
            return ctx.enter_context(nc.sbuf_tensor(name, shape, dt))

        def sem(name):
            return ctx.enter_context(nc.semaphore(name))

        x = sb("x", [P, B * NT, D])
        tm = sb("tm", [P, B * NT, D])
        fm = sb("fm", [P, B, T])
        xb = sb("xb", [P, B * NT, D])
        rows = sb("rows", [sum(n for _, n in COLUMNS), P])
        col = sb("col", [P, sum(n for _, n in COLUMNS)])
        colx = sb("colx", [P, 8])
        bc = sb("bc", [P, len(BROADCASTS), D])
        w = {n: sb("w_" + n, [P, c]) for n, c in WEIGHTS}
        ident = sb("ident", [P, P])
        identb = sb("identb", [P, P], BF16)
        mask = sb("mask", [P, T])
        junk = sb("junk", [P, 2, T])
        nhalf = sb("nhalf", [P, NT])
        ctx_a = sb("ctx_a", [P, B, D])
        ctx_b = sb("ctx_b", [SB, B, D])
        ctx_t = sb("ctx_t", [P, B * S])
        q_stack = sb("q_stack", [P, QR, 4, T], BF16)
        k_stack = sb("k_stack", [P, 2, PAIRS, T], BF16)
        kc_stack = sb("kc_stack", [P, 2, PAIRS, B * S], BF16)
        v_self = sb("v_self", [P, 2, NT, H, DH + 1])
        vc_a = sb("vc_a", [P, 2, B, H, DH + 1])
        vc_b = sb("vc_b", [P, 2, B, GROUPS, DH + 1])
        E = sb("E", [P, 4, 4, T])
        raw = sb("raw", [P, 2, B * S])
        rem = sb("rem", [P, 2, B * S])
        parts = sb("parts", [P, 2, 3, B * S], BF16)
        one_head_ctx = kc_stack[:, :, :, :].rearrange("p l a t -> p (l a t)").bitcast(F32)
        kc_t = one_head_ctx[:, 0:2 * B * S].rearrange("p (l t) -> p l t", l=2)
        vcd_a = one_head_ctx[:, 2 * B * S:2 * B * S + 2 * T].rearrange("p (l b d) -> p l b d", l=2, d=D)
        vcd_b = one_head_ctx[0:SB, 2 * B * S + 2 * T:2 * B * S + 4 * T]\
            .rearrange("p (l b d) -> p l b d", l=2, d=D)
        acc_s = sb("acc_s", [P, 2, T])
        mx = sb("mx", [P, 2, NT, 4])
        mxc = sb("mxc", [P, 2, NT, 4])
        nm = sb("nm", [P, 2, NT, 2, 4], BF16)
        nmr = sb("nmr", [P, 2, NT, 4])
        nmt = sb("nmt", [8, 2, T], BF16)
        rden = sb("rden", [P, 2, NT, 4])
        st = sb("st", [P, B, NT, 6])
        mv = sb("mv", [P, B, NT, 2])
        ve = sb("ve", [P, B, NT])
        rs = sb("rs", [P, B, NT])
        nmx = sb("nmx", [P, B, NT])
        rsum = sb("rsum", [P, B, NT])
        rinv = sb("rinv", [P, B, NT])

        psum = ctx.enter_context(nc.psum_tensor("psum", [P, 8, T], F32))
        BANKS = {"A": (0, 2), "B": (2, 4), "S0": (4, 5), "S1": (5, 6), "ACC": (6, 7), "MISC": (7, 8)}
        ONE = ("S0", "S1", "ACC", "MISC")

        def bank(u):
            a, z = BANKS[u]
            return psum[:, a:z, :].rearrange("p a t -> p (a t)")

        q_scratch = nc.dram_tensor("q_scratch", (3 * B, P, TERMS, T), BF16).ap()
        k_scratch = nc.dram_tensor("k_scratch", (2 * B, P, TERMS, T), BF16).ap()
        kc_scratch = nc.dram_tensor("kc_scratch", (2, P, TERMS, B * S), BF16).ap()

        c0, at_col = 0, {}
        for name, n in COLUMNS:
            at_col[name] = c0
            c0 += n
        NCOL = c0
        at_bc = {name: i for i, (name, _) in enumerate(BROADCASTS)}

        def colv(name, i=0):
            return col[:, at_col[name] + i:at_col[name] + i + 1]

        def bcv(name):
            return bc[:, at_bc[name], :]

        def bct(name):
            return bc[:, at_bc[name]:at_bc[name] + 1, :].to_broadcast([P, NT, D])

        def tiles(buf, b):
            return buf[:, NT * b:NT * b + NT, :]

        filled = {u: sem("bank_filled_" + u) for u in BANKS}
        freed = {u: sem("bank_freed_" + u) for u in BANKS}
        x_loaded = [sem(f"x_loaded{b}") for b in range(B)]
        ctx_loaded = sem("ctx_loaded")
        rows_loaded = sem("rows_loaded")
        bc_loaded = sem("bc_loaded")
        w_loaded = [sem(f"w_loaded{i}") for i in range(3)]
        consts = sem("consts")
        ones_rows = sem("ones_rows")
        v_ones = sem("v_ones")
        colx_ready = sem("colx_ready")
        rem_ready = sem("rem_ready")
        mid_ready = sem("mid_ready")
        parts_ready = sem("parts_ready")
        bounced = [sem(f"bounced{i}") for i in range(2)]
        kc_stacked = [sem(f"kc_stacked{i}") for i in range(2)]
        q_zeroed = sem("q_zeroed")
        q_stacked = [sem(f"q_stacked{i}") for i in range(QR)]
        k_stacked = [sem(f"k_stacked{i}") for i in range(2)]
        max_joined = sem("max_joined")
        nm_step = sem("nm_step")
        nm_ready = sem("nm_ready")
        neg_rows = [sem(f"neg_rows{i}") for i in range(2)]
        mask_done = sem("mask_done")
        slot_read = sem("slot_read")
        rden_ready = sem("rden_ready")
        stats_done = [sem(f"stats_done{k}") for k in range(NORMS)]
        moments = [sem(f"moments{k}") for k in range(NORMS)]
        var_eps = [sem(f"var_eps{k}") for k in range(NORMS)]
        rstd_ready = [sem(f"rstd_ready{k}") for k in range(NORMS)]
        hat_ready = [sem(f"hat_ready{k}") for k in range(NORMS)]
        affined = {k: sem("affined_" + k) for k in ("n2", "m1", "m2", "c1", "c2", "f")}
        x_biased = {k: sem("x_biased_" + k) for k in ("b2", "bo1", "bo2", "bff2", "m", "c")}
        x_attended = sem("x_attended")
        sig_ready = sem("sig_ready")
        gate_ready = sem("gate_ready")
        gated = sem("gated")
        dmaxed = sem("dmaxed")
        rinv_ready = sem("rinv_ready")
        h2_ready = sem("h2_ready")
        h2_added = sem("h2_added")
        stored = sem("stored")

        turn = {}
        uses = {u: 0 for u in BANKS}

        def claim(pe, u, key):
            if uses[u]:
                pe.wait_ge(freed[u], uses[u])
            uses[u] += 1
            turn[key] = (u, uses[u])
            return bank(u)

        def await_bank(eng, key):
            u, n = turn[key]
            eng.wait_ge(filled[u], n)
            return bank(u)

        def frees(key):
            return freed[turn[key][0]]

        def await_taken(eng, key):
            u, n = turn[key]
            eng.wait_ge(freed[u], n)

        OPERANDS = [("kc", 0), ("kc", 1)]
        for a in (CAUSAL, SELF, CROSS):
            for b in range(B):
                OPERANDS.append(("q", a, b))
                if a != CROSS:
                    OPERANDS.append(("k", a, b))
        op_no = {k: i for i, k in enumerate(OPERANDS)}
        slot_no, slot_reader, mask_no = {}, [], {}

        def add_slot(key, reader):
            slot_no[key] = len(slot_reader)
            slot_reader.append(reader)

        reads = {}
        for a in (CAUSAL, SELF, CROSS):
            for n in range(B * GROUPS):
                for kt in KEY_TILES[a]:
                    add_slot((a, n, kt), ("acc", a, n) if kt == KEY_TILES[a][-1] else None)
                    if slot_reader[-1] is None:
                        reads[len(slot_reader) - 1] = len(reads) + 1
                    if a == CAUSAL and kt not in ("A", "B"):
                        mask_no[(a, n, kt)] = len(mask_no) + 1
            if a != SELF:
                for b in range(B):
                    add_slot(("ffn", a, b), ("ffn", a, b))
        for a in ("m", "c", "d"):
            for b in range(B):
                add_slot(("P", a, b), ("pt", a, b, 3 if a == "m" else 1))
                add_slot(("PT", a, b), ("pv", a, b))

        def slot(key):
            return E[:, slot_no[key] % 4]

        def await_slot(eng, key):
            e = slot_no[key] - 4
            if e < 0:
                return
            if slot_reader[e] is None:
                eng.wait_ge(slot_read, reads[e])
            else:
                await_bank(eng, slot_reader[e])

        def s_units(a):
            res = []
            for pair in range(2):
                items = []
                if a != CROSS:
                    items += [("self", 3), ("self", 2), ("self", 1), ("self", 0)]
                if a != SELF:
                    items += [("ctx", 0), ("ctx", 2)]
                for it in items:
                    for par in range(2):
                        res.append((2 * pair + par, *it))
            return res

        def keys_seen(a, qt):
            return (qt + 1) * P if a == CAUSAL else T

        NG = B * GROUPS
        KEYS = {"m": T, "c": S, "d": S}

        def first_query(a, kt):
            return kt * P if a == CAUSAL and kt not in ("A", "B") else 0

        def one_head(b):
            if b < 2:
                return q_stack[:, 2 * b:2 * b + 2, :, :].rearrange("p g a t -> p (g a t)").bitcast(F32)
            return k_stack[:, b % 2, :, :].rearrange("p a t -> p (a t)").bitcast(F32)

        def await_x(eng, what, b):
            if what == "in":
                eng.wait_ge(x_loaded[b], 16)
            elif what == "att":
                eng.wait_ge(x_attended, b + 1)
            elif what in ("m", "c", "f"):
                eng.wait_ge(affined["f" if what == "f" else what + "2"], 2 * b + 2)
            else:
                await_taken(eng, {"b2": ("ffn", CAUSAL, b), "bo1": ("wo", SELF, b),
                                  "bo2": ("wo", CROSS, b), "bff2": ("ffn", CROSS, b)}[what])

        def steps(a, n):
            kts = KEY_TILES[a]
            st = [(kt, h) for kt in kts for h in ((0,) if kt == "B" else (0, 1))]
            st = st if 0 <= n < NG else [None]
            units = s_units(a) if -2 <= n < NG - 2 else []
            nq, nk = (n + 6) // GROUPS, (n + 5) // GROUPS
            jobs = {}

            def job(i, what, m):
                if what not in ("k", "v") or a != CROSS:
                    jobs.setdefault(min(i, len(st) - 1), []).append((what, m))

            if n == -3:
                job(0, "q", 0)
                job(0, "k", 0)
                job(0, "v", 0)
            if n >= -2 and (n + 6) % GROUPS == 0 and nq < B:
                job(0, "q", nq)
            if -1 <= n < NG - 1:
                job(1, "nm", n + 1)
            if n >= -2 and (n + 5) % GROUPS == 0 and nk < B:
                job(2, "k", nk)
            if n >= 1:
                job(3, "out", n - 1)
            if n >= 0 and n % GROUPS == 0 and n // GROUPS + 1 < B:
                job(4, "v", n // GROUPS + 1)
            res = []
            for i, step in enumerate(st):
                part = units[len(units) * i // len(st):len(units) * (i + 1) // len(st)]
                values = None
                if step and (step[1] == 1 or step[0] == "B") and step[0] != kts[0]:
                    values = kts[kts.index(step[0]) - 1]
                res.append((step, part, values, jobs.get(i, [])))
            return res

        def splits(a, n):
            return [j for _, _, _, jobs in steps(a, n) for j in jobs if j[0] in ("q", "k")]

        def load_weight(eng, name):
            src = inp[name]
            n = [m for m, _ in WEIGHTS].index(name)
            dst = w[name][:, :]
            if src.shape[0] > P:
                src = src.rearrange("(c p) d -> p c d", p=P)
                dst = dst.rearrange("p (c d) -> p c d", d=D)
            eng.dma_start(dst, src).then_inc(w_loaded[0 if n < 2 else 1 if n < FIRST_WEIGHTS else 2], 16)

        block = ctx.enter_context(nc.Block())

        def pe_setup(pe):
            pe.wait_ge(rows_loaded, 16 * len(COLUMNS))
            pe.wait_ge(consts, 6)
            ps = claim(pe, "S0", "col")
            pe.transpose(ps[:, 0:NCOL], rows[:, :], ident[0:NCOL, 0:NCOL]).then_inc(filled["S0"], 1)
            pe.wait_ge(ctx_loaded, 32)
            for key, u, src, n in (("ctxA", "S1", ctx_a, P), ("ctxB", "ACC", ctx_b, SB)):
                ps = claim(pe, u, key)
                for b in range(B):
                    mm = pe.transpose(ps[:, b * n:(b + 1) * n], src[:, b, :], ident[0:n, 0:n])
                mm.then_inc(filled[u], 1)
            pe.wait_ge(w_loaded[0], 16 * 2)
            await_taken(pe, "ctxA")
            await_taken(pe, "ctxB")
            for i, wn in enumerate(("L0_xattn_w_ckv", "L1_xattn_Wkv2")):
                pe_context_keys(pe, ("kc", i), "AB"[i], w[wn][:, 0:D])
                pe_context_values(pe, ("vcA", i), ("vcB", i), i, w[wn][:, D:2 * D], 4)

        def pe_setup_one_head(pe):
            pe.wait_ge(w_loaded[2], 16 * (len(WEIGHTS) - FIRST_WEIGHTS))
            for i, (wk, wv) in enumerate((("L2_xattn_wk_c", "L2_xattn_wv_c"),
                                          ("L3_xattn_Wk", "L3_xattn_Wv"))):
                pe_context_keys(pe, ("kd", i), "AB"[i], w[wk][:, :])
                pe_context_values(pe, ("vdA", i), ("vdB", i), i, w[wv][:, :], 1)

        def pe_context_keys(pe, key, u, wk):
            ps = claim(pe, u, key)
            pe.matmul(ps[:, 0:T], wk, ctx_t[:, 0:T], start=True, stop=True)
            pe.matmul(ps[:, T:B * S], wk, ctx_t[:, T:B * S], start=True, stop=True)\
              .then_inc(filled[u], 1)

        def pe_context_values(pe, key_a, key_b, i, wv, copies):
            u = ("S0", "ACC")[i]
            ps = claim(pe, u, key_a)
            for b in range(B):
                mm = pe.matmul(ps[:, b * D:(b + 1) * D], ctx_t[:, b * S:b * S + P], wv,
                               start=True, stop=True)
            mm.then_inc(filled[u], 1)
            u = ("S1", "MISC")[i]
            ps = claim(pe, u, key_b)
            for b in range(B):
                for j in range(copies):
                    mm = pe.matmul(ps[32 * j:32 * j + SB, b * D:(b + 1) * D],
                                   ctx_t[:, b * S + P:(b + 1) * S], wv,
                                   start=True, stop=True, tile_position=(0, 32 * j))
            mm.then_inc(filled[u], 1)

        def pe_turn(pe, k, b, src):
            u = ONE[b]
            ps = claim(pe, u, ("turn", k, b))
            for t in range(NT):
                mm = pe.transpose(ps[:, t * P:(t + 1) * P], src[:, NT * b + t, :], ident[:, :])
            mm.then_inc(filled[u], 1)

        def pe_turn_hat(pe, k, b):
            pe.wait_ge(hat_ready[k], b + 1)
            pe_turn(pe, k, b, tm)

        PROJ = {CAUSAL: (0, ("L0_xattn_w_qkv", 0), ("L0_xattn_w_qkv", D), ("L0_xattn_w_qkv", 2 * D)),
                SELF: (3, ("L1_xattn_Wq1", 0), ("L1_xattn_Wkv1", 0), ("L1_xattn_Wkv1", D)),
                CROSS: (4, ("L1_xattn_Wq2", 0), None, None)}

        def pe_project(pe, a, b, what):
            await_taken(pe, ("turn", PROJ[a][0], b))
            name, o = PROJ[a][1 + "qkv".index(what)]
            ps = claim(pe, "MISC", (what, a, b))
            if what == "v":
                for t in range(NT):
                    mm = pe.matmul(ps[:, t * D:(t + 1) * D], fm[:, b, t * P:(t + 1) * P],
                                   w[name][:, o:o + D], start=True, stop=True)
            else:
                mm = pe.matmul(ps[:, :], w[name][:, o:o + D], fm[:, b, :], start=True, stop=True)
            mm.then_inc(filled["MISC"], 1)

        def pe_scores_for_max(pe, a, n, units):
            b, g = divmod(n, GROUPS)
            l = 0 if a == CAUSAL else 1
            c = NG * a + n
            if units[0] == s_units(a)[0]:
                pe.wait_ge(q_stacked[c % QR], STACKED * (c // QR + 1))
            if g == 0 and units[0] == s_units(a)[0]:
                if a != CROSS:
                    pe.wait_ge(k_stacked[b % 2], STACKED * ((B * a + b) // 2 + 1))
                if a != SELF:
                    pe.wait_ge(kc_stacked[l], STACKED)
            for j, what, i in units:
                h = 4 * g + j
                pair = h // 2
                u = "S0" if h % 2 == 0 else "S1"
                ps = claim(pe, u, ("S", a, n, j, what, i))
                q = q_stack[0:NEG, c % QR, j, :]
                if what == "self":
                    m = keys_seen(a, i)
                    pe.matmul(ps[:, 0:m], q[:, i * P:(i + 1) * P],
                              k_stack[0:NEG, b % 2, pair, 0:m],
                              start=True, stop=True).then_inc(filled[u], 1)
                else:
                    for qt in (i, i + 1):
                        mm = pe.matmul(ps[:, (qt - i) * S:(qt - i + 1) * S], q[:, qt * P:(qt + 1) * P],
                                       kc_stack[0:NEG, l, pair, b * S:(b + 1) * S],
                                       start=True, stop=True)
                    mm.then_inc(filled[u], 1)

        def pe_turn_max(pe, a, n):
            c = NG * a + n
            pe.wait_ge(nm_ready, c + 1)
            ps = claim(pe, "MISC", ("nm", a, n))
            for t in range(NT):
                mm = pe.transpose(ps[0:8, t * P // 2:(t + 1) * P // 2].bitcast(BF16),
                                  nm[:, c % 2, t, :, :].rearrange("p k j -> p (k j)"), identb[:, :])
            mm.then_inc(filled["MISC"], 1)

        def pe_shifted_scores(pe, a, n, kt, half):
            b, g = divmod(n, GROUPS)
            c = NG * a + n
            l = 0 if a == CAUSAL else 1
            if kt == KEY_TILES[a][0] and half == 0:
                pe.wait_ge(neg_rows[c % 2], NEG_ROWS * (c // 2 + 1))
            u = "AB"[half]
            ps = claim(pe, u, ("ST", a, n, kt, half))
            q0 = first_query(a, kt)
            for j in (range(4) if kt == "B" else (2 * half, 2 * half + 1)):
                h = 4 * g + j
                pair, at = h // 2, (j % 2) * T
                q = q_stack[:, c % QR, j, q0:T]
                if kt == "B":
                    mm = pe.matmul(ps[32 * j:32 * j + SB, 0:T], kc_stack[:, l, pair, b * S + P:(b + 1) * S], q,
                                   start=True, stop=True, tile_position=(0, 32 * j))
                else:
                    k = (kc_stack[:, l, pair, b * S:b * S + P] if kt == "A"
                         else k_stack[:, b % 2, pair, kt * P:(kt + 1) * P])
                    mm = pe.matmul(ps[:, at:at + T - q0], k, q, start=True, stop=True)
            mm.then_inc(filled[u], 1)

        def pe_weighted_values(pe, a, n, kt):
            b, g = divmod(n, GROUPS)
            l = 0 if a == CAUSAL else 1
            e = slot((a, n, kt))
            first, last = kt == KEY_TILES[a][0], kt == KEY_TILES[a][-1]
            if first:
                claim(pe, "ACC", ("acc", a, n))
                if a != CROSS and g == 0:
                    await_taken(pe, ("v", a, b))
                if n == 0 and a != SELF:
                    await_taken(pe, ("vcA", l))
                    await_taken(pe, ("vcB", l))
            for half in ((0,) if kt == "B" else (0, 1)):
                await_taken(pe, ("ST", a, n, kt, half))
            if (a, n, kt) in mask_no:
                pe.wait_ge(mask_done, mask_no[(a, n, kt)])
            ps = bank("ACC")
            q0 = first_query(a, kt)
            for j in range(4):
                h = 4 * g + j
                o = ps[32 * j:32 * j + DH + 1, q0:T]
                if kt == "B":
                    rr = slice(32 * j, 32 * j + SB)
                    mm = pe.matmul(o, vc_b[rr, l, b, g, :], e[rr, 0, :], start=first, stop=last,
                                   tile_position=(32 * j, 32 * j), skip_group_check=True)
                else:
                    v = vc_a[:, l, b, h, :] if kt == "A" else v_self[:, b % 2, kt, h, :]
                    mm = pe.matmul(o, v, e[:, j, 0:T - q0], start=first, stop=last,
                                   tile_position=(0, 32 * j), skip_group_check=True)
            mm.then_inc(filled["ACC"] if last else slot_read, 1)

        def pe_turn_out(pe, a, n):
            await_taken(pe, ("acc", a, n))
            ps = claim(pe, "MISC", ("out", a, n))
            for t in range(NT):
                mm = pe.transpose(ps[:, t * P:(t + 1) * P],
                                  acc_s[:, (NG * a + n) % 2, t * P:(t + 1) * P], ident[:, :])
            mm.then_inc(filled["MISC"], 1)

        def pe_attention(pe, a):
            for n in range(-3, NG + 1):
                for step, units, values, extras in steps(a, n):
                    if step:
                        pe_shifted_scores(pe, a, n, *step)
                    if units:
                        pe_scores_for_max(pe, a, n + 2, units)
                    if values is not None:
                        pe_weighted_values(pe, a, n, values)
                    for what, m in extras:
                        if what == "nm":
                            pe_turn_max(pe, a, m)
                        elif what == "out":
                            pe_turn_out(pe, a, m)
                        else:
                            pe_project(pe, a, m, what)
                if 0 <= n < NG:
                    pe_weighted_values(pe, a, n, KEY_TILES[a][-1])

        def pe_after_attention(pe, a, k, name):
            for b in range(B):
                await_taken(pe, ("out", a, GROUPS * b + GROUPS - 1))
                pe_turn(pe, k, b, tm)
            for b in range(B):
                await_taken(pe, ("turn", k, b))
                pe_token_major(pe, ("wo", a, b), b, fm[:, b, :], name)

        def pe_token_major(pe, key, b, src, name):
            u = ONE[b]
            ps = claim(pe, u, key)
            for t in range(NT):
                mm = pe.matmul(ps[:, t * D:(t + 1) * D], src[:, t * P:(t + 1) * P], w[name][:, :],
                               start=True, stop=True)
            mm.then_inc(filled[u], 1)

        def pe_hidden(pe, a, k, b):
            await_taken(pe, ("turn", k, b))
            name = "L0_xattn_w1" if a == CAUSAL else "L1_xattn_Wff1"
            for c in range(2 if a == CAUSAL else FC):
                u = "AB"[c % 2]
                ps = claim(pe, u, ("hid", a, b, c))
                for i, m in enumerate((2 * c, 2 * c + 1) if a == CAUSAL else (c, FC + c)):
                    mm = pe.matmul(ps[:, i * T:(i + 1) * T], w[name][:, m * P:(m + 1) * P],
                                   fm[:, b, :], start=True, stop=True)
                mm.then_inc(filled[u], 1)

        def pe_ffn_out(pe, a, b):
            name = "L0_xattn_w2" if a == CAUSAL else "L1_xattn_Wff2"
            if a == CAUSAL:
                await_taken(pe, ("hid", a, b, 0))
                await_taken(pe, ("hid", a, b, 1))
            else:
                for c in (2, 3):
                    await_taken(pe, ("hid", a, b, c))
            u = ONE[b]
            ps = claim(pe, u, ("ffn", a, b))
            hid = slot(("ffn", a, b))
            for t in range(NT):
                for c in range(FC):
                    mm = pe.matmul(ps[:, t * D:(t + 1) * D], hid[:, c, t * P:(t + 1) * P],
                                   w[name][:, c * D:(c + 1) * D], start=(c == 0), stop=(c == FC - 1))
            mm.then_inc(filled[u], 1)

        ONE_HEAD = {"m": (7, "L2_xattn_wq_m"), "c": (8, "L2_xattn_wq_c"), "d": (10, "L3_xattn_Wq")}

        def pe_turn_x(pe, k, b):
            await_x(pe, {7: "bff2", 8: "m", 9: "c", 10: "f"}[k], b)
            pe_turn(pe, k, b, x)

        def pe_project_one_head(pe, a, b):
            k, wq = ONE_HEAD[a]
            await_taken(pe, ("turn", k, b))
            names = [("qd", wq)] + ([("kd_", "L2_xattn_wk_m")] if a == "m" else [])
            for what, wn in names:
                u = ONE[(b + 1) % 4] if what == "qd" else ONE[(b + 2) % 4]
                ps = claim(pe, u, (what, a, b))
                pe.matmul(ps[:, :], w[wn][:, :], fm[:, b, :], start=True, stop=True)\
                  .then_inc(filled[u], 1)
            if a == "m":
                pe_token_major(pe, ("vd_", a, b), b, fm[:, b, :], "L2_xattn_wv_m")

        def pe_one_head_scores(pe, a, b):
            q = one_head(b)[:, 0:T]
            await_taken(pe, ("qd", a, b))
            if a == "m":
                await_taken(pe, ("kd_", a, b))
                k = one_head(b)[:, T:2 * T]
            else:
                k = kc_t[:, a == "d", b * S:(b + 1) * S]
            for half in range(2):
                u = "AB"[half]
                ps = claim(pe, u, ("Sd", a, b, half))
                for i in range(2):
                    t = 2 * half + i
                    mm = pe.matmul(ps[:, i * T:i * T + KEYS[a]], q[:, t * P:(t + 1) * P], k,
                                   start=True, stop=True)
                mm.then_inc(filled[u], 1)

        def pe_turn_probs(pe, a, b):
            e = slot(("P", a, b))
            for half in range(2):
                await_taken(pe, ("Sd", a, b, half))
            if a == "m":
                for t in range(NT):
                    ps = claim(pe, ONE[t], ("pt", a, b, t))
                    for kt in range(NT):
                        mm = pe.transpose(ps[:, kt * P:(kt + 1) * P], e[:, t, kt * P:(kt + 1) * P],
                                          ident[:, :])
                    mm.then_inc(filled[ONE[t]], 1)
            else:
                for i, (k0, m) in enumerate(((0, P), (P, SB))):
                    u = ONE[(2 * b + i) % 4]
                    ps = claim(pe, u, ("pt", a, b, i))
                    for t in range(NT):
                        mm = pe.transpose(ps[0:m, t * P:(t + 1) * P], e[:, t, k0:k0 + m], ident[:, :])
                    mm.then_inc(filled[u], 1)

        def pe_one_head_values(pe, a, b):
            pt = slot(("PT", a, b))
            u = ONE[(2 * b + 2) % 4]
            for t in range(4 if a == "m" else 2):
                await_taken(pe, ("pt", a, b, t))
            if a == "m":
                await_taken(pe, ("vd_", a, b))
                v = one_head(b)[:, 2 * T:3 * T]
            else:
                await_taken(pe, ("vdA", int(a == "d")))
                await_taken(pe, ("vdB", int(a == "d")))
            ps = claim(pe, u, ("pv", a, b))
            for t in range(NT):
                o = ps[:, t * D:(t + 1) * D]
                if a == "m":
                    for kt in range(NT):
                        mm = pe.matmul(o, pt[:, t, kt * P:(kt + 1) * P], v[:, kt * D:(kt + 1) * D],
                                       start=(kt == 0), stop=(kt == NT - 1))
                else:
                    pe.matmul(o, pt[:, 0, t * P:(t + 1) * P], vcd_a[:, a == "d", b, :],
                              start=True, stop=False)
                    mm = pe.matmul(o, pt[0:SB, 1, t * P:(t + 1) * P], vcd_b[:, a == "d", b, :],
                                   start=False, stop=True)
            mm.then_inc(filled[u], 1)

        def pe_one_head_attention(pe, a):
            for b in range(B):
                pe_turn_x(pe, ONE_HEAD[a][0], b)
            for b in range(B):
                pe_project_one_head(pe, a, b)
            for b in range(B + 1):
                if b < B:
                    pe_one_head_scores(pe, a, b)
                if b >= 1:
                    pe_turn_probs(pe, a, b - 1)
                    pe_one_head_values(pe, a, b - 1)

        @block.tensor
        def _(pe):
            pe_setup(pe)
            pe.wait_ge(w_loaded[1], 16 * (FIRST_WEIGHTS - 2))
            for b in range(B):
                pe_turn_hat(pe, 0, b)
            pe_attention(pe, CAUSAL)
            for b in range(B):
                pe_turn_hat(pe, 2, b)
            for b in range(B):
                pe_hidden(pe, CAUSAL, 2, b)
                if b >= 1:
                    pe_ffn_out(pe, CAUSAL, b - 1)
            pe_ffn_out(pe, CAUSAL, B - 1)
            for b in range(B):
                pe_turn_hat(pe, 3, b)
            pe_attention(pe, SELF)
            pe_after_attention(pe, SELF, 11, "L1_xattn_Wo1")
            for b in range(B):
                pe_turn_hat(pe, 4, b)
            pe_attention(pe, CROSS)
            pe_setup_one_head(pe)
            pe_after_attention(pe, CROSS, 12, "L1_xattn_Wo2")
            for b in range(B):
                pe_turn_hat(pe, 5, b)
            for b in range(B):
                pe_hidden(pe, CROSS, 5, b)
                if b >= 1:
                    pe_ffn_out(pe, CROSS, b - 1)
            pe_ffn_out(pe, CROSS, B - 1)
            pe_one_head_attention(pe, "m")
            pe_one_head_attention(pe, "c")
            for b in range(B):
                pe_turn_x(pe, 9, b)
            for b in range(B):
                await_taken(pe, ("turn", 9, b))
                ps = claim(pe, ONE[b], ("h1", b))
                pe.matmul(ps[:, :], w["L2_xattn_f0_w"][:, :], fm[:, b, :], start=True, stop=True)\
                  .then_inc(filled[ONE[b]], 1)
            for b in range(B):
                await_taken(pe, ("h1", b))
                pe_token_major(pe, ("h2", b), b, one_head(b)[:, 0:T], "L2_xattn_f1_w")
            pe_one_head_attention(pe, "d")

        IDN = ACT.Identity

        def act_raw(act, key, scale, bias):
            o = op_no[key]
            ps = await_bank(act, key)
            m = B * S if key[0] == "kc" else T
            if o >= 2:
                act.wait_ge(bounced[o % 2], BOUNCED * (o // 2))
            act.activation(raw[:, o % 2, 0:m], ps[:, 0:m], IDN, bias=bias, scale=scale)
            act.activation(parts[:, o % 2, 0, 0:m], ps[:, 0:m], IDN, bias=bias, scale=scale)\
               .then_inc(frees(key), 1)

        def act_project(act, a, b, what):
            if what == "q":
                bias = colx[:, 0:1] if a == CAUSAL else 0.0
                act_raw(act, ("q", a, b), HEAD_SCALE[a], bias)
            elif what == "k":
                act_raw(act, ("k", a, b), 1.0, colv("L0_xattn_b_qkv", 1) if a == CAUSAL else 0.0)

        def act_setup(act):
            ps = await_bank(act, "col")
            act.copy(col[:, :], ps[:, 0:NCOL]).then_inc(frees("col"), 1)
            ct = ctx_t[:, :].rearrange("p (b s) -> p b s", s=S)
            for key, k0, m in (("ctxA", 0, P), ("ctxB", P, SB)):
                ps = await_bank(act, key)
                act.copy(ct[:, :, k0:k0 + m], ps[:, 0:B * m].rearrange("p (b s) -> p b s", s=m))\
                   .then_inc(frees(key), 1)
            await_taken(act, "col")
            act_raw(act, ("kc", 0), 1.0, colv("L0_xattn_b_ckv"))
            act_raw(act, ("kc", 1), 1.0, 0.0)

        def act_setup_one_head(act):
            for i in range(2):
                ps = await_bank(act, ("kd", i))
                act.activation(kc_t[:, i, :], ps[:, 0:B * S], IDN,
                               bias=colv("L2_xattn_bk_c") if i == 0 else 0.0).then_inc(frees(("kd", i)), 1)

        def act_turn(act, k, b, gain=None, plus=None):
            key = ("turn", k, b)
            ps = await_bank(act, key)
            if gain:
                act.activation(fm[:, b, :], ps[:, :], IDN, bias=colv(plus), scale=colv(gain))\
                   .then_inc(frees(key), 1)
            else:
                act.copy(fm[:, b, :], ps[:, :]).then_inc(frees(key), 1)

        def act_exp(act, a, n, kt, half):
            key = ("ST", a, n, kt, half)
            ps = await_bank(act, key)
            e = slot((a, n, kt))
            if half == 0:
                await_slot(act, (a, n, kt))
            m = T - first_query(a, kt)
            if kt == "B":
                ex = act.activation(e[:, 0, :], ps[:, 0:T], ACT.Exp)
            else:
                pv = ps.rearrange("p (j t) -> p j t", j=2)
                ex = act.activation(e[:, 2 * half:2 * half + 2, 0:m], pv[:, :, 0:m], ACT.Exp)
            ex.then_inc(frees(key), 1)

        def act_attention(act, a):
            for n in range(-3, NG + 1):
                for i, (step, units, values, extras) in enumerate(steps(a, n)):
                    if step:
                        act_exp(act, a, n, *step)
                    if i == 0 and n >= 1:
                        ps = await_bank(act, ("acc", a, n - 1))
                        act.copy(acc_s[:, (NG * a + n - 1) % 2, :], ps).then_inc(frees(("acc", a, n - 1)), 1)
                    for what, m in extras:
                        if what == "nm":
                            ps = await_bank(act, ("nm", a, m))
                            act.copy(nmt[:, (NG * a + m) % 2, :], ps[0:8, 0:T // 2].bitcast(BF16))\
                               .then_inc(frees(("nm", a, m)), 1)
                        elif what != "out":
                            act_project(act, a, m, what)

        def act_one_head(act, a):
            k, _ = ONE_HEAD[a]
            ai = "mcd".index(a)
            for b in range(B):
                act_turn(act, k, b)
            for b in range(B):
                ps = await_bank(act, ("qd", a, b))
                act.activation(one_head(b)[:, 0:T], ps, IDN,
                               bias=0.0 if a == "d" else colx[:, 1 + ai:2 + ai],
                               scale=float(D) ** -0.5 if a == "d" else 0.125).then_inc(frees(("qd", a, b)), 1)
                if a == "m":
                    ps = await_bank(act, ("kd_", a, b))
                    act.activation(one_head(b)[:, T:2 * T], ps, IDN, bias=colv("L2_xattn_bk_m"))\
                       .then_inc(frees(("kd_", a, b)), 1)
            for b in range(B + 1):
                if b < B:
                    await_slot(act, ("P", a, b))
                    e = slot(("P", a, b))
                    for half in range(2):
                        act.wait_ge(dmaxed, 2 * (ai * B + b) + half + 1)
                        ps = await_bank(act, ("Sd", a, b, half))
                        for i in range(2):
                            t = 2 * half + i
                            ex = act.activation(e[:, t, 0:KEYS[a]], ps[:, i * T:i * T + KEYS[a]], ACT.Exp,
                                                bias=nmx[:, b, t:t + 1], accum_out=rsum[:, b, t:t + 1])
                        ex.then_inc(frees(("Sd", a, b, half)), 1)
                if b >= 1:
                    await_slot(act, ("PT", a, b - 1))
                    pt = slot(("PT", a, b - 1))
                    for t in ((0, 2) if a == "m" else (0,)):
                        key = ("pt", a, b - 1, t)
                        ps = await_bank(act, key)
                        act.copy(pt[:, t, :], ps).then_inc(frees(key), 1)

        def act_hidden(act, a):
            for b in range(B):
                if a == CAUSAL:
                    await_slot(act, ("ffn", a, b))
                    hid = slot(("ffn", a, b))
                    for c in range(2):
                        ps = await_bank(act, ("hid", a, b, c))
                        for i in range(2):
                            m = 2 * c + i
                            g = act.activation(hid[:, m, :], ps[:, i * T:(i + 1) * T], ACT.Gelu,
                                               bias=colv("L0_xattn_b1", m))
                        g.then_inc(frees(("hid", a, b, c)), 1)
                else:
                    for c in range(FC):
                        ps = await_bank(act, ("hid", a, b, c))
                        act.activation(raw[:, c % 2, 0:T], ps[:, T:2 * T], ACT.Sigmoid,
                                       bias=colx[:, 3 + c:4 + c], scale=1.702).then_inc(sig_ready, 1)

        @block.scalar
        def _(act):
            for name, _ in WEIGHTS[2:]:
                load_weight(act, name)
            for i, (name, o) in enumerate(BROADCASTS):
                act.dma_start(bc[:, i, :], inp[name][o:o + D].partition_broadcast(P)).then_inc(bc_loaded, 16)
            act_setup(act)
            for b in range(B):
                act_turn(act, 0, b, "L0_xattn_g1", "L0_xattn_be1")
            act.wait_ge(colx_ready, 4)
            act_attention(act, CAUSAL)
            for b in range(B):
                act_turn(act, 2, b, "L0_xattn_gf", "L0_xattn_bf")
            act_hidden(act, CAUSAL)
            for b in range(B):
                act_turn(act, 3, b, "L1_xattn_ln1_s", "L1_xattn_ln1_b")
            act_attention(act, SELF)
            for b in range(B):
                act_turn(act, 11, b)
            for b in range(B):
                act_turn(act, 4, b, "L1_xattn_ln2_s", "L1_xattn_ln2_b")
            act_attention(act, CROSS)
            act_setup_one_head(act)
            for b in range(B):
                act_turn(act, 12, b)
            for b in range(B):
                act_turn(act, 5, b, "L1_xattn_ln3_s", "L1_xattn_ln3_b")
            act_hidden(act, CROSS)
            act_one_head(act, "m")
            act_one_head(act, "c")
            for b in range(B):
                act_turn(act, 9, b)
            for b in range(B):
                ps = await_bank(act, ("h1", b))
                act.activation(one_head(b)[:, 0:T], ps, ACT.Gelu, bias=colv("L2_xattn_f0_b"))\
                   .then_inc(frees(("h1", b)), 1)
            for b in range(B):
                await_taken(act, ("h2", b))
                act.activation(tiles(tm, b), tiles(tm, b), ACT.Gelu).then_inc(h2_ready, 1)
            act_one_head(act, "d")

        def dve_stats(dve, k, b, src):
            for t in range(NT):
                i = dve.bn_stats(st[:, b, t, :], src[:, NT * b + t, :])
            i.then_inc(stats_done[k], 1)
            dve.wait_ge(stats_done[k], b + 1)
            for t in range(NT):
                i = dve.bn_aggr(mv[:, b, t, :], st[:, b, t, :])
            i.then_inc(moments[k], 1)

        def dve_hat(dve, k, b, src):
            dve.wait_ge(rstd_ready[k], b + 1)
            for t in range(NT):
                i = dve.tensor_scalar(tm[:, NT * b + t, :], src[:, NT * b + t, :], mv[:, b, t, 0:1],
                                      rs[:, b, t:t + 1], ALU.subtract, ALU.mult)
            i.then_inc(hat_ready[k], 1)

        def dve_norms(dve, k, src, ready, after=None):
            for b in range(B + 1):
                if b < B:
                    ready(b)
                    dve_stats(dve, k, b, src)
                if b >= 1:
                    dve_hat(dve, k, b - 1, src)
                    if after:
                        dve.wait_ge(hat_ready[k], b)
                        after(b - 1)

        def dve_affine(dve, key, b, dst, gain, plus):
            dve.tensor_tensor(tiles(tm, b), tiles(tm, b), bct(gain), ALU.mult).then_inc(affined[key], 1)
            dve.wait_ge(affined[key], 2 * b + 1)
            dve.tensor_tensor(tiles(dst, b), tiles(tm, b), plus, ALU.add).then_inc(affined[key], 1)

        def dve_scores_max(dve, a, n, units):
            b, g = divmod(n, GROUPS)
            c = (NG * a + n) % 2
            for j, what, i in units:
                key = ("S", a, n, j, what, i)
                ps = await_bank(dve, key)
                if what == "ctx":
                    r = dve.tensor_reduce(mxc[:, c, i:i + 2, j], ps[:, 0:2 * S].rearrange("p (t s) -> p t s", s=S),
                                          AX.X, ALU.max)
                elif a == CAUSAL:
                    m = keys_seen(a, i)
                    r = dve.tensor_tensor_reduce(junk[:, j % 2, 0:m], ps[:, 0:m], mask[:, T - m:T], 1.0, LOWEST,
                                                 ALU.add, ALU.max, mx[:, c, i, j:j + 1])
                else:
                    r = dve.tensor_reduce(mx[:, c, i, j:j + 1], ps, AX.X, ALU.max)
                r.then_inc(frees(key), 1)
            if a == CAUSAL and units and units[-1] == s_units(a)[-1]:
                for j in (2, 3):
                    await_taken(dve, ("S", a, n, j, "ctx", 2))
                dve.tensor_tensor(mx[:, c, :, :], mx[:, c, :, :], mxc[:, c, :, :], ALU.max).then_inc(max_joined, 1)

        def dve_out(dve, a, n):
            b, g = divmod(n, GROUPS)
            c = NG * a + n
            key = ("out", a, n)
            ps = await_bank(dve, key).rearrange("p (t j e) -> p t j e", t=NT, e=32)
            dve.reciprocal(rden[:, c % 2, :, :], ps[:, :, :, DH]).then_inc(rden_ready, 1)
            dve.wait_ge(rden_ready, c + 1)
            o = tiles(tm, b)[:, :, 32 * g:32 * g + 32].rearrange("p t (j d) -> p t j d", d=DH)
            dve.tensor_tensor(o, ps[:, :, :, 0:DH],
                              rden[:, c % 2, :, :].unsqueeze(3).to_broadcast([P, NT, 4, DH]), ALU.mult)\
               .then_inc(frees(key), 1)
            if a == CAUSAL and g == GROUPS - 1:
                await_taken(dve, key)
                dve.tensor_tensor(tiles(x, b), tiles(x, b), tiles(tm, b), ALU.add).then_inc(x_attended, 1)

        def dve_values(dve, a, b):
            key = ("v", a, b)
            ps = await_bank(dve, key).rearrange("p (t h d) -> p t h d", t=NT, d=DH)
            o = v_self[:, b % 2, :, :, 0:DH]
            if a == CAUSAL:
                bias = bcv("L0_xattn_b_qkv").rearrange("p (h d) -> p h d", d=DH).unsqueeze(1)
                dve.tensor_tensor(o, ps, bias.to_broadcast([P, NT, H, DH]), ALU.add).then_inc(frees(key), 1)
            else:
                dve.tensor_copy(o, ps).then_inc(frees(key), 1)

        def dve_mid(dve, key):
            o = op_no[key]
            m = B * S if key[0] == "kc" else T
            dve.wait_ge(rem_ready, o + 1)
            dve.tensor_copy(parts[:, o % 2, 1, 0:m], rem[:, o % 2, 0:m]).then_inc(mid_ready, 1)

        def dve_attention(dve, a):
            for n in range(-3, NG + 1):
                for step, units, values, extras in steps(a, n):
                    dve_scores_max(dve, a, n + 2, units)
                    for what, m in extras:
                        if what == "out":
                            dve_out(dve, a, m)
                        elif what == "v":
                            dve_values(dve, a, m)
                for what, m in splits(a, n):
                    dve_mid(dve, (what, a, m))

        def dve_setup(dve):
            dve.memset(q_stack[:].rearrange("p g a t -> p (g a t)").bitcast(F32), 0.0).then_inc(q_zeroed, 1)
            for buf in (v_self, vc_a, vc_b):
                dve.memset(buf[:], 1.0).then_inc(v_ones, 1)
            dve.wait_ge(v_ones, 3)
            dve.wait_ge(bc_loaded, 16 * len(BROADCASTS))
            for i in range(2):
                if i == 0:
                    dve_mid(dve, ("kc", 0))
                bias = bcv("L0_xattn_b_ckv")
                ps = await_bank(dve, ("vcA", i)).rearrange("p (b h d) -> p b h d", b=B, d=DH)
                o = vc_a[:, i, :, :, 0:DH]
                if i == 0:
                    bb = bias.rearrange("p (h d) -> p h d", d=DH).unsqueeze(1).to_broadcast([P, B, H, DH])
                    r = dve.tensor_tensor(o, ps, bb, ALU.add)
                else:
                    r = dve.tensor_copy(o, ps)
                r.then_inc(frees(("vcA", i)), 1)
                ps = await_bank(dve, ("vcB", i)).rearrange("p (b g j d) -> p b g j d", b=B, g=GROUPS, d=DH)
                for j in range(4):
                    rr = slice(32 * j, 32 * j + SB)
                    o = vc_b[rr, i, :, :, 0:DH]
                    if i == 0:
                        bb = bias[rr, :].rearrange("p (g j d) -> p g j d", g=GROUPS, d=DH)[:, :, j, :]
                        r = dve.tensor_tensor(o, ps[rr, :, :, j, :],
                                              bb.unsqueeze(1).to_broadcast([SB, B, GROUPS, DH]), ALU.add)
                    else:
                        r = dve.tensor_copy(o, ps[rr, :, :, j, :])
                r.then_inc(frees(("vcB", i)), 1)
            dve_mid(dve, ("kc", 1))

        def dve_setup_one_head(dve):
            for i in range(2):
                for key, buf, m in ((("vdA", i), vcd_a, P), (("vdB", i), vcd_b, SB)):
                    ps = await_bank(dve, key)[0:m, :].rearrange("p (b d) -> p b d", d=D)
                    if i == 0:
                        bias = bc[0:m, at_bc["L2_xattn_bv_c"]:at_bc["L2_xattn_bv_c"] + 1, :]
                        r = dve.tensor_tensor(buf[:, i, :, :], ps, bias.to_broadcast([m, B, D]), ALU.add)
                    else:
                        r = dve.tensor_copy(buf[:, i, :, :], ps)
                    r.then_inc(frees(key), 1)

        def dve_residual(dve, key, b, biased):
            ps = await_bank(dve, key).rearrange("p (t d) -> p t d", d=D)
            dve.wait_ge(x_biased[biased], b + 1)
            dve.tensor_tensor(tiles(x, b), ps, tiles(xb, b), ALU.add).then_inc(frees(key), 1)

        def dve_one_head(dve, a):
            ai = "mcd".index(a)
            if a == "m":
                for b in range(B):
                    ps = await_bank(dve, ("vd_", a, b)).rearrange("p (t d) -> p t d", d=D)
                    o = one_head(b)[:, 2 * T:3 * T].rearrange("p (t d) -> p t d", d=D)
                    dve.tensor_tensor(o, ps, bct("L2_xattn_bv_m"), ALU.add).then_inc(frees(("vd_", a, b)), 1)
            for b in range(B + 1):
                if b < B:
                    for half in range(2):
                        ps = await_bank(dve, ("Sd", a, b, half)).rearrange("p (i t) -> p i t", i=2)
                        dve.tensor_reduce(nmx[:, b, 2 * half:2 * half + 2], ps[:, :, 0:KEYS[a]], AX.X, ALU.max,
                                          negate=True).then_inc(dmaxed, 1)
                if b >= 1:
                    await_slot(dve, ("PT", a, b - 1))
                    pt = slot(("PT", a, b - 1))
                    for t in ((1, 3) if a == "m" else (1,)):
                        key = ("pt", a, b - 1, t)
                        ps = await_bank(dve, key)
                        m = P if a == "m" else SB
                        dve.tensor_copy(pt[0:m, t, :], ps[0:m, :]).then_inc(frees(key), 1)
                    for half in range(2):
                        await_taken(dve, ("Sd", a, b - 1, half))
                    dve.reciprocal(rinv[:, b - 1, :], rsum[:, b - 1, :]).then_inc(rinv_ready, 1)
                    dve.wait_ge(rinv_ready, ai * B + b)
                    key = ("pv", a, b - 1)
                    ps = await_bank(dve, key)
                    for t in range(NT):
                        i = NT * (b - 1) + t
                        r = dve.scalar_tensor_tensor(out=tm[:, i, :], in0=ps[:, t * D:(t + 1) * D],
                                                     scalar=rinv[:, b - 1, t:t + 1], in1=x[:, i, :],
                                                     op0=ALU.mult, op1=ALU.add)
                    r.then_inc(frees(key), 1)
            if a == "d":
                return
            k = 6 + 2 * ai

            def inner(b):
                dve.wait_ge(x_biased[a], b + 1)
                dve_affine(dve, a + "1", b, tm, f"L2_xattn_g_{a}", tiles(xb, b))

            dve_norms(dve, k, tm, lambda b: await_taken(dve, ("pv", a, b)), inner)
            dve_norms(dve, k + 1, tm, lambda b: dve.wait_ge(affined[a + "1"], 2 * b + 2),
                      lambda b: dve_affine(dve, a + "2", b, x, "L2_xattn_g_d", bct("L2_xattn_b_d")))

        @block.vector
        def _(dve):
            dve_setup(dve)
            dve_norms(dve, 0, x, lambda b: await_x(dve, "in", b))
            dve.wait_ge(consts, 7)
            dve_attention(dve, CAUSAL)
            dve_norms(dve, 1, x, lambda b: await_x(dve, "att", b),
                      lambda b: dve_affine(dve, "n2", b, xb, "L0_xattn_g2", bct("L0_xattn_be2")))
            dve_norms(dve, 2, xb, lambda b: dve.wait_ge(affined["n2"], 2 * b + 2))
            for b in range(B):
                dve_residual(dve, ("ffn", CAUSAL, b), b, "b2")
            dve_norms(dve, 3, x, lambda b: await_x(dve, "b2", b))
            dve_attention(dve, SELF)
            for b in range(B):
                dve_residual(dve, ("wo", SELF, b), b, "bo1")
            dve_norms(dve, 4, x, lambda b: await_x(dve, "bo1", b))
            dve_attention(dve, CROSS)
            dve_setup_one_head(dve)
            for b in range(B):
                dve_residual(dve, ("wo", CROSS, b), b, "bo2")
            dve_norms(dve, 5, x, lambda b: await_x(dve, "bo2", b))
            for b in range(B + 1):
                if b < B:
                    await_slot(dve, ("ffn", CROSS, b))
                    hid = slot(("ffn", CROSS, b))
                    for c in range(FC):
                        m = FC * b + c + 1
                        ps = await_bank(dve, ("hid", CROSS, b, c))
                        dve.wait_ge(sig_ready, m)
                        dve.scalar_tensor_tensor(out=rem[:, c % 2, 0:T], in0=ps[:, T:2 * T],
                                                 scalar=colv("L1_xattn_bff1", FC + c), in1=raw[:, c % 2, 0:T],
                                                 op0=ALU.add, op1=ALU.mult).then_inc(gated, 1)
                        dve.wait_ge(gated, m)
                        dve.scalar_tensor_tensor(out=hid[:, c, :], in0=ps[:, 0:T],
                                                 scalar=colv("L1_xattn_bff1", c), in1=rem[:, c % 2, 0:T],
                                                 op0=ALU.add, op1=ALU.mult)\
                           .then_inc(frees(("hid", CROSS, b, c)), 1)
                if b >= 1:
                    dve_residual(dve, ("ffn", CROSS, b - 1), b - 1, "bff2")
            dve_one_head(dve, "m")
            dve_one_head(dve, "c")
            for b in range(B):
                ps = await_bank(dve, ("h2", b)).rearrange("p (t d) -> p t d", d=D)
                dve.tensor_tensor(tiles(tm, b), ps, bct("L2_xattn_f1_b"), ALU.add).then_inc(frees(("h2", b)), 1)
            for b in range(B):
                dve.wait_ge(h2_ready, b + 1)
                dve.tensor_tensor(tiles(tm, b), tiles(tm, b), tiles(x, b), ALU.add).then_inc(h2_added, 1)
            dve_norms(dve, 10, tm, lambda b: dve.wait_ge(h2_added, b + 1),
                      lambda b: dve_affine(dve, "f", b, x, "L2_xattn_g_d", bct("L2_xattn_b_d")))
            dve_one_head(dve, "d")

        def pool_rstd(pool, k):
            for b in range(B):
                pool.wait_ge(moments[k], b + 1)
                pool.tensor_scalar(ve[:, b, :], mv[:, b, :, 1], EPS, None, ALU.add).then_inc(var_eps[k], 1)
                pool.wait_ge(var_eps[k], b + 1)
                pool.tensor_tensor(rs[:, b, :], ve[:, b, :], nhalf[:, :], ALU.pow).then_inc(rstd_ready[k], 1)

        def pool_bias(pool, key, after, name):
            for b in range(B):
                await_x(pool, after, b)
                if key == "b2":
                    pool.wait_ge(hat_ready[2], b + 1)
                pool.tensor_tensor(tiles(xb, b), tiles(x, b), bct(name), ALU.add).then_inc(x_biased[key], 1)

        def pool_rem(pool, key):
            o = op_no[key]
            m = B * S if key[0] == "kc" else T
            await_taken(pool, key)
            pool.tensor_tensor(rem[:, o % 2, 0:m], raw[:, o % 2, 0:m], parts[:, o % 2, 0, 0:m], ALU.subtract)\
                .then_inc(rem_ready, 1)

        def pool_low(pool, key):
            o = op_no[key]
            m = B * S if key[0] == "kc" else T
            pool.wait_ge(mid_ready, o + 1)
            pool.tensor_tensor(parts[:, o % 2, 2, 0:m], rem[:, o % 2, 0:m], parts[:, o % 2, 1, 0:m], ALU.subtract)\
                .then_inc(parts_ready, 1)

        def pool_minus_max(pool, a, n):
            c = NG * a + n
            if a == CAUSAL:
                pool.wait_ge(max_joined, n + 1)
            else:
                last = s_units(a)[-1]
                for j in (2, 3):
                    await_taken(pool, ("S", a, n, j, last[1], last[2]))
            m = (mxc if a == CROSS else mx)[:, c % 2, :, :]
            hi, lo, r = nm[:, c % 2, :, 0, :], nm[:, c % 2, :, 1, :], nmr[:, c % 2, :, :]
            pool.tensor_scalar(hi, m, -1.0, None, ALU.mult).then_inc(nm_step, 1)
            pool.wait_ge(nm_step, 2 * c + 1)
            pool.tensor_tensor(r, m, hi, ALU.add).then_inc(nm_step, 1)
            pool.wait_ge(nm_step, 2 * c + 2)
            pool.tensor_scalar(lo, r, -1.0, None, ALU.mult).then_inc(nm_ready, 1)

        def pool_attention(pool, a):
            for n in range(-3, NG + 1):
                if -1 <= n < NG - 1:
                    pool_minus_max(pool, a, n + 1)
                todo = splits(a, n)
                for kt in (KEY_TILES[a] if 0 <= n < NG else ()):
                    if (a, n, kt) in mask_no:
                        for half in range(2):
                            await_taken(pool, ("ST", a, n, kt, half))
                        e = slot((a, n, kt))[:, :, 0:P]
                        pool.affine_select(out=e, in_=e, compare_op=ALU.is_ge, fill=0.0, base=0,
                                           pattern=[[0, 4], [1, P]], channel_multiplier=-1)\
                            .then_inc(mask_done, 1)
                    if todo and kt in (1, 2):
                        pool_rem(pool, (todo[0][0], a, todo[0][1]))
                        todo = todo[1:]
                for what, m in todo:
                    pool_rem(pool, (what, a, m))
                for what, m in splits(a, n):
                    pool_low(pool, (what, a, m))

        @block.gpsimd
        def _(pool):
            pool.memset(ident[:, :], 0.0).then_inc(consts, 1)
            pool.memset(identb[:, :], 0.0).then_inc(consts, 1)
            pool.memset(mask[:, :], 0.0).then_inc(consts, 1)
            pool.wait_ge(consts, 3)
            for m in (ident, identb):
                pool.affine_select(out=m[:, :], in_=m[:, :], compare_op=ALU.not_equal, fill=1.0, base=0,
                                   pattern=[[-1, P]], channel_multiplier=1).then_inc(consts, 1)
            tri = mask[:, T - P:T]
            pool.affine_select(out=tri, in_=tri, compare_op=ALU.is_ge, fill=MASKED, base=0,
                               pattern=[[-1, P]], channel_multiplier=1).then_inc(consts, 1)
            pool.memset(nhalf[:, :], -0.5).then_inc(consts, 1)
            pool.wait_ge(consts, 7)
            for buf in (kc_stack, k_stack):
                pool.memset(buf[NEG:P].rearrange("p l a t -> p (l a t)").bitcast(F32), ONES).then_inc(ones_rows, 1)
            pool.wait_ge(ones_rows, 2)
            await_taken(pool, "col")
            for i, (src, m, f) in enumerate(((colv("L0_xattn_b_qkv"), 1, HEAD_SCALE[CAUSAL]),
                                             (colv("L2_xattn_bq_m"), 1, 0.125), (colv("L2_xattn_bq_c"), 1, 0.125),
                                             (col[:, at_col["L1_xattn_bff1"] + FC:at_col["L1_xattn_bff1"] + 2 * FC],
                                              FC, 1.702))):
                pool.tensor_scalar(colx[:, i:i + m], src, f, None, ALU.mult).then_inc(colx_ready, 1)
            pool.wait_ge(consts, 7)
            pool_rem(pool, ("kc", 0))
            pool_rem(pool, ("kc", 1))
            pool_low(pool, ("kc", 0))
            pool_low(pool, ("kc", 1))
            pool_rstd(pool, 0)
            pool.wait_ge(bc_loaded, 16 * len(BROADCASTS))
            pool_attention(pool, CAUSAL)
            pool_rstd(pool, 1)
            pool_rstd(pool, 2)
            pool_bias(pool, "b2", "att", "L0_xattn_b2")
            pool_rstd(pool, 3)
            pool_bias(pool, "bo1", "b2", "L1_xattn_bo1")
            pool_attention(pool, SELF)
            pool_rstd(pool, 4)
            pool_bias(pool, "bo2", "bo1", "L1_xattn_bo2")
            pool_attention(pool, CROSS)
            pool_rstd(pool, 5)
            pool_bias(pool, "bff2", "bo2", "L1_xattn_bff2")
            pool_bias(pool, "m", "bff2", "L2_xattn_b_m")
            pool_rstd(pool, 6)
            pool_rstd(pool, 7)
            pool_bias(pool, "c", "m", "L2_xattn_b_c")
            pool_rstd(pool, 8)
            pool_rstd(pool, 9)
            pool_rstd(pool, 10)

        def sp_parts_out(sp, key, dram, runs, m):
            o = op_no[key]
            sp.wait_ge(parts_ready, o + 1)
            for slot0, n, part, same in runs:
                src = parts[:, o % 2, part:part + (1 if same else n), 0:m]
                sp.dma_start(dram[:, slot0:slot0 + n, :], src.to_broadcast([P, n, m]) if same else src)\
                  .then_inc(bounced[o % 2], 16)

        def sp_stack_in(sp, o, dram, stack, done):
            sp.wait_ge(bounced[o % 2], BOUNCED * (o // 2 + 1))
            src = dram.rearrange("(pr par r) k t -> par (r k) pr t", par=2, r=DH)
            for par in range(2):
                sp.dma_start(stack(par), src[par]).then_inc(done, 16)

        def sp_keys_in(sp, a, b):
            if b >= 2:
                await_bank(sp, ("acc", a, GROUPS * (b - 1) - 1))
            elif a == SELF:
                await_bank(sp, ("acc", CAUSAL, GROUPS * (b + 3) - 1))
            sp_stack_in(sp, op_no[("k", a, b)], k_scratch[B * a + b],
                        lambda par: k_stack[KR * par:KR * par + KR, b % 2, :, :], k_stacked[b % 2])

        def sp_queries_in(sp, a, n):
            c = NG * a + n
            b, g = divmod(n, GROUPS)
            if c >= QR:
                a2, n2 = divmod(c - QR, NG)
                last = KEY_TILES[a2][-1]
                await_bank(sp, ("ST", a2, n2, last, 0 if last == "B" else 1))
            sp_stack_in(sp, op_no[("q", a, b)], q_scratch[B * a + b, 4 * g * DH:4 * (g + 1) * DH],
                        lambda par: q_stack[KR * par:KR * par + KR, c % QR, par::2, :], q_stacked[c % QR])

        def sp_attention(sp, a):
            for n in range(-3, NG + 1):
                if -1 <= n < NG - 1:
                    c = NG * a + n + 1
                    await_taken(sp, ("nm", a, n + 1))
                    for k in range(2):
                        sp.dma_start(q_stack[NEG + k:NEG + k + 1, c % QR, :, :], nmt[4 * k:4 * k + 4, c % 2, :])\
                          .then_inc(neg_rows[c % 2], 16)
                for what, b in splits(a, n):
                    dram = q_scratch[B * a + b] if what == "q" else k_scratch[B * a + b]
                    sp_parts_out(sp, (what, a, b), dram, Q_RUNS if what == "q" else K_RUNS, T)
                if n == -3:
                    for g in range(2):
                        sp_queries_in(sp, a, g)
                    if a != CROSS:
                        sp_keys_in(sp, a, 0)
                    for g in range(2, 4):
                        sp_queries_in(sp, a, g)
                elif 4 <= n + 5 < NG:
                    sp_queries_in(sp, a, n + 5)
                if a != CROSS and n > -3 and (n + 5) % GROUPS == 0 and (n + 5) // GROUPS < B:
                    sp_keys_in(sp, a, (n + 5) // GROUPS)

        @block.sync
        def _(sp):
            for name, n in COLUMNS:
                src = inp[name][0:n * P].rearrange("(n p) -> n p", p=P)
                sp.dma_start(rows[at_col[name]:at_col[name] + n, :], src).then_inc(rows_loaded, 16)
            sp.dma_start(ctx_a[:, :, :], inp["ctx_1024"][:, 0:P, :].rearrange("b p d -> p b d")).then_inc(ctx_loaded, 16)
            sp.dma_start(ctx_b[:, :, :], inp["ctx_1024"][:, P:S, :].rearrange("b p d -> p b d")).then_inc(ctx_loaded, 16)
            for name, _ in WEIGHTS[0:2]:
                load_weight(sp, name)
            for b in range(B):
                sp.dma_start(tiles(x, b), inp["x"][b].rearrange("(t p) d -> p t d", p=P)).then_inc(x_loaded[b], 16)
            sp.wait_ge(ones_rows, 2)
            for l in range(2):
                sp_parts_out(sp, ("kc", l), kc_scratch[l], K_RUNS, B * S)
                sp_stack_in(sp, op_no[("kc", l)], kc_scratch[l],
                            lambda par: kc_stack[KR * par:KR * par + KR, l, :, :], kc_stacked[l])
            sp.wait_ge(q_zeroed, 1)
            sp_attention(sp, CAUSAL)
            sp_attention(sp, SELF)
            sp_attention(sp, CROSS)
            for b in range(B):
                await_taken(sp, ("pv", "d", b))
                sp.dma_start(out[b].rearrange("(t p) d -> p t d", p=P), tiles(tm, b)).then_inc(stored, 16)
            sp.wait_ge(stored, 16 * B)


def kernel(**inputs):
    import numpy as np
    import concourse.bacc as bacc
    from concourse.bass_utils import run_bass_kernel_spmd

    nc = bacc.Bacc("TRN2", target_bir_lowering=False, num_devices=1)
    arrays, aps = {}, {}
    for name, value in inputs.items():
        a = np.ascontiguousarray(value)
        arrays[f"in_{name}"] = a
        aps[name] = nc.dram_tensor(f"in_{name}", a.shape, mybir.dt.from_np(a.dtype), kind="ExternalInput").ap()
    out = nc.dram_tensor("out_x", (B, T, D), F32, kind="ExternalOutput").ap()
    four_cross_attention_blocks(nc, out, **aps)
    got = run_bass_kernel_spmd(nc, [arrays], core_ids=[0])
    return got.results[0]["out_x"]
```

```python
from contextlib import ExitStack

import concourse.bass as bass
from concourse import mybir

F32 = mybir.dt.float32
BF16 = mybir.dt.bfloat16
ALU = mybir.AluOpType
ACT = mybir.ActivationFunctionType
AX = mybir.AxisListType

P = 128
B, T, D = 4, 512, 128
S = 154
SB = S - P
KB = 32
NT = T // P
H, DH = 16, 8
PAIRS = H // 2
GROUPS = H // 4
TERMS = 6
KR = TERMS * DH
NEG = P - 2
Q_RUNS = ((0, 3, 0, True), (3, 2, 1, True), (5, 1, 2, True))
K_RUNS = ((0, 3, 0, False), (3, 2, 0, False), (5, 1, 0, False))
QR = 6
ONES = 1.0019378662109375
FC = 4
EPS = 1e-5
NORMS = 11
LOWEST = -3.0e38
MASKED = -1.0e30
STACKED = 16 * 2
BOUNCED = 16 * len(Q_RUNS)
NEG_ROWS = 16 * 2

CAUSAL, SELF, CROSS = 0, 1, 2
KEY_TILES = {CAUSAL: (0, 1, 2, 3, "A", "B"), SELF: (0, 1, 2, 3), CROSS: ("A", "B")}
HEAD_SCALE = {CAUSAL: float(DH) ** -0.5, SELF: 0.125, CROSS: 0.125}

ROUNDS = 3 * B * (H // 4)

COLUMNS = [
    ("L0_xattn_b_qkv", 3), ("L0_xattn_g1", 1), ("L0_xattn_be1", 1), ("L0_xattn_b_ckv", 2),
    ("L0_xattn_gf", 1), ("L0_xattn_bf", 1), ("L0_xattn_b1", 4),
    ("L1_xattn_ln1_s", 1), ("L1_xattn_ln1_b", 1), ("L1_xattn_ln2_s", 1), ("L1_xattn_ln2_b", 1),
    ("L1_xattn_ln3_s", 1), ("L1_xattn_ln3_b", 1), ("L1_xattn_bff1", 8),
    ("L2_xattn_bq_m", 1), ("L2_xattn_bk_m", 1), ("L2_xattn_bq_c", 1), ("L2_xattn_bk_c", 1),
    ("L2_xattn_f0_b", 1),
]
FIRST_COLUMNS = 4
FIRST_ROWS = sum(n for _, n in COLUMNS[0:FIRST_COLUMNS])
ALL_ROWS = sum(n for _, n in COLUMNS)
BROADCASTS = [
    ("L0_xattn_b_qkv", 2 * D), ("L0_xattn_b_ckv", D), ("L0_xattn_g2", 0), ("L0_xattn_be2", 0),
    ("L0_xattn_b2", 0), ("L1_xattn_bo1", 0), ("L1_xattn_bo2", 0), ("L1_xattn_bff2", 0),
    ("L2_xattn_bv_m", 0), ("L2_xattn_g_m", 0), ("L2_xattn_b_m", 0), ("L2_xattn_bv_c", 0),
    ("L2_xattn_g_c", 0), ("L2_xattn_b_c", 0), ("L2_xattn_f1_b", 0), ("L2_xattn_g_d", 0),
    ("L2_xattn_b_d", 0),
]
WEIGHTS = [
    ("L0_xattn_w_qkv", 3 * D), ("L0_xattn_w_ckv", 2 * D),
    ("L0_xattn_w1", 4 * D), ("L0_xattn_w2", 4 * D), ("L1_xattn_Wkv2", 2 * D),
    ("L1_xattn_Wq1", D), ("L1_xattn_Wkv1", 2 * D), ("L1_xattn_Wo1", D), ("L1_xattn_Wq2", D),
    ("L1_xattn_Wo2", D), ("L1_xattn_Wff1", 8 * D), ("L1_xattn_Wff2", 4 * D),
    ("L2_xattn_wk_c", D), ("L2_xattn_wv_c", D), ("L3_xattn_Wk", D), ("L3_xattn_Wv", D),
    ("L2_xattn_wq_m", D), ("L2_xattn_wk_m", D), ("L2_xattn_wv_m", D),
    ("L2_xattn_wq_c", D), ("L2_xattn_f0_w", D), ("L2_xattn_f1_w", D), ("L3_xattn_Wq", D),
]
WEIGHT_SETS = (0, 2, 12, len(WEIGHTS))
BROADCAST_SETS = (0, 2, len(BROADCASTS))


def four_cross_attention_blocks(nc: bass.Bass, out: bass.AP, **inp: bass.AP):
    with ExitStack() as ctx:
        def sb(name, shape, dt=F32):
            return ctx.enter_context(nc.sbuf_tensor(name, shape, dt))

        def sem(name):
            return ctx.enter_context(nc.semaphore(name))

        x = sb("x", [P, B * NT, D])
        tm = sb("tm", [P, B * NT, D])
        fm = sb("fm", [P, B, T])
        xb = sb("xb", [P, B * NT, D])
        rows = [sb(f"rows{i}", [n, P]) for i, n in enumerate((FIRST_ROWS, ALL_ROWS - FIRST_ROWS))]
        col = sb("col", [P, ALL_ROWS])
        colx = sb("colx", [P, 8])
        bc = sb("bc", [P, len(BROADCASTS), D])
        w = {n: sb("w_" + n, [P, c]) for n, c in WEIGHTS}
        ident = sb("ident", [P, P])
        identb = sb("identb", [P, P], BF16)
        mask = sb("mask", [P, T])
        junk = sb("junk", [P, 3, T])
        nhalf = sb("nhalf", [P, NT])
        ctx_a = sb("ctx_a", [P, B, D])
        ctx_b = sb("ctx_b", [SB, B, D])
        ctx_t = sb("ctx_t", [P, B * S])
        q_stack = sb("q_stack", [P, QR, 4, T], BF16)
        k_stack = sb("k_stack", [P, 2, PAIRS, T], BF16)
        kc_stack = sb("kc_stack", [P, 2, PAIRS, B * S], BF16)
        v_self = sb("v_self", [P, 2, NT, H, DH + 1])
        vc_a = sb("vc_a", [P, 2, B, H, DH + 1])
        vc_b = sb("vc_b", [P, 2, B, GROUPS, DH + 1])
        E = sb("E", [P, 4, 4, T])
        split = sb("split", [P, 2, 2, B * S])
        raw, rem = split[:, 0], split[:, 1]
        parts = sb("parts", [P, 2, 3, B * S], BF16)
        def words(buf):
            return buf.rearrange("p l a t -> p (l a t)")

        tail = [words(k_stack[:, 0:1]).bitcast(F32), words(k_stack[:, 1:2]).bitcast(F32),
                words(split[:, :]), words(q_stack[:, 0:2]).bitcast(F32)]
        probs_m = [words(buf).bitcast(F32)[:, 0:NT * T].rearrange("p (t k) -> p t k", t=NT)
                   for buf in (kc_stack[:, 0:1], kc_stack[:, 1:2], q_stack[:, 2:4], q_stack[:, 4:6])]
        acc_s = sb("acc_s", [P, 2, T])
        mx = sb("mx", [P, 2, NT, 4])
        mxc = sb("mxc", [P, 2, NT, 4])
        nm = sb("nm", [P, 2, NT, 2, 4], BF16)
        nmr = sb("nmr", [P, 2, NT, 4])
        nmt = sb("nmt", [8, 2, T], BF16)
        rden = sb("rden", [P, 2, NT, 4])
        st = sb("st", [P, B, NT, 6])
        mv = sb("mv", [P, B, NT, 2])
        ve = sb("ve", [P, B, NT])
        rs = sb("rs", [P, B, NT])
        nmx = sb("nmx", [P, B, NT])
        rsum = sb("rsum", [P, B, NT])
        rinv = sb("rinv", [P, B, NT])

        psum = ctx.enter_context(nc.psum_tensor("psum", [P, 8, T], F32))
        BANKS = {"A": (0, 2), "B": (2, 4), "S0": (4, 5), "S1": (5, 6), "ACC": (6, 7), "MISC": (7, 8)}

        def bank(u):
            a, z = BANKS[u]
            return psum[:, a:z, :].rearrange("p a t -> p (a t)")

        q_scratch = nc.dram_tensor("q_scratch", (3 * B, P, TERMS, T), BF16).ap()
        k_scratch = nc.dram_tensor("k_scratch", (2 * B, P, TERMS, T), BF16).ap()
        kc_scratch = nc.dram_tensor("kc_scratch", (2, P, TERMS, B * S), BF16).ap()

        c0, at_col = 0, {}
        for name, n in COLUMNS:
            at_col[name] = c0
            c0 += n
        at_bc = {name: i for i, (name, _) in enumerate(BROADCASTS)}

        def colv(name, i=0):
            return col[:, at_col[name] + i:at_col[name] + i + 1]

        def bcv(name):
            return bc[:, at_bc[name], :]

        def bct(name):
            return bc[:, at_bc[name]:at_bc[name] + 1, :].to_broadcast([P, NT, D])

        def tiles(buf, b):
            return buf[:, NT * b:NT * b + NT, :]

        filled = {u: sem("bank_filled_" + u) for u in BANKS}
        freed = {u: sem("bank_freed_" + u) for u in BANKS}
        x_loaded = [sem(f"x_loaded{b}") for b in range(B)]
        ctx_loaded = sem("ctx_loaded")
        rows_loaded = [sem(f"rows_loaded{i}") for i in range(2)]
        bc_loaded = [sem(f"bc_loaded{i}") for i in range(2)]
        w_loaded = [sem(f"w_loaded{i}") for i in range(3)]
        consts = sem("consts")
        ones_rows = sem("ones_rows")
        v_ones = sem("v_ones")
        once_only = sem("once_only")
        colx_ready = sem("colx_ready")
        rem_ready = sem("rem_ready")
        mid_ready = sem("mid_ready")
        parts_ready = sem("parts_ready")
        bounced = [sem(f"bounced{i}") for i in range(2)]
        kc_stacked = [sem(f"kc_stacked{i}") for i in range(2)]
        q_zeroed = sem("q_zeroed")
        q_stacked = [sem(f"q_stacked{i}") for i in range(QR)]
        k_stacked = [sem(f"k_stacked{i}") for i in range(2)]
        max_joined = sem("max_joined")
        nm_step = sem("nm_step")
        nm_ready = sem("nm_ready")
        neg_rows = [sem(f"neg_rows{i}") for i in range(2)]
        mask_done = sem("mask_done")
        slot_read = sem("slot_read")
        rden_ready = sem("rden_ready")
        stats_done = [sem(f"stats_done{k}") for k in range(NORMS)]
        moments = [sem(f"moments{k}") for k in range(NORMS)]
        var_eps = [sem(f"var_eps{k}") for k in range(NORMS)]
        rstd_ready = [sem(f"rstd_ready{k}") for k in range(NORMS)]
        hat_ready = [sem(f"hat_ready{k}") for k in range(NORMS)]
        affined = {k: sem("affined_" + k) for k in ("n2", "m1", "m2", "c1", "c2", "f")}
        x_biased = {k: sem("x_biased_" + k) for k in ("b2", "bo1", "bo2", "bff2", "m", "c")}
        x_attended = sem("x_attended")
        sig_ready = sem("sig_ready")
        dmaxed = sem("dmaxed")
        rinv_ready = sem("rinv_ready")
        h2_ready = sem("h2_ready")
        h2_added = sem("h2_added")
        stored = sem("stored")

        turn = {}
        uses = {u: 0 for u in BANKS}

        def claim(pe, u, key):
            if uses[u]:
                pe.wait_ge(freed[u], uses[u])
            uses[u] += 1
            turn[key] = (u, uses[u])
            return bank(u)

        def await_bank(eng, key):
            u, n = turn[key]
            eng.wait_ge(filled[u], n)
            return bank(u)

        def frees(key):
            return freed[turn[key][0]]

        def await_taken(eng, key):
            u, n = turn[key]
            eng.wait_ge(freed[u], n)

        slot_no, slot_reader, mask_no = {}, [], {}

        def add_slot(key, reader):
            slot_no[key] = len(slot_reader)
            slot_reader.append(reader)

        reads = {}

        def slot(key):
            return E[:, slot_no[key] % 4]

        def await_slot(eng, key):
            e = slot_no[key] - 4
            if e < 0:
                return
            if slot_reader[e] is None:
                eng.wait_ge(slot_read, reads[e])
            else:
                await_bank(eng, slot_reader[e])

        def s_units(a):
            res = []
            for pair in range(2):
                items = []
                if a != CROSS:
                    items += [("self", 3), ("self", 2), ("self", 1), ("self", 0)]
                if a != SELF:
                    items += [("ctx", 0), ("ctx", 2)]
                for it in items:
                    for par in range(2):
                        res.append((2 * pair + par, *it))
            return res

        def keys_seen(a, qt):
            return (qt + 1) * P if a == CAUSAL else T

        NG = B * GROUPS
        KEYS = {"m": T, "c": S, "d": S}

        def first_query(a, kt):
            return kt * P if a == CAUSAL and kt not in ("A", "B") else 0

        def await_x(eng, what, b):
            if what == "in":
                eng.wait_ge(x_loaded[b], 16)
            elif what == "att":
                eng.wait_ge(x_attended, b + 1)
            elif what in ("m", "c", "f"):
                eng.wait_ge(affined["f" if what == "f" else what + "2"], b + 1)
            else:
                await_taken(eng, {"b2": ("ffn", CAUSAL, b), "bo1": ("wo", SELF, b),
                                  "bo2": ("wo", CROSS, b), "bff2": ("ffn", CROSS, b)}[what])

        STEP_LENGTH = {CAUSAL: 1.82, SELF: 0.81, CROSS: 2.434}
        LAST_LENGTH = 0.72
        Q_STEP, K_STEP, V_STEP, NM_STEP, OUT_STEP = 1, 1, 4, 0, 9
        MID_WAIT = 3.45
        CHAIN_SCALE = {CAUSAL: 1.6, SELF: 0.899}
        TAIL_SCALE = (0.816, 0.694, 0.816, 0.816)
        TAIL_START = ((42, 1), (46, 0), (47, 0), (47, 0))
        STEPS = []

        def step_columns(step):
            if step is None:
                return 1
            a, _, kt, _ = step
            return 700 + (T if kt == "B" else 2 * (T - first_query(a, kt)))

        def unit_columns(a, unit):
            return 2 * S if unit[1] == "ctx" else keys_seen(a, unit[2])

        def plan_rounds():
            for c in range(-3, ROUNDS + 1):
                a, n = divmod(c, NG)
                kts = KEY_TILES[a] if 0 <= c < ROUNDS else ()
                st = [(a, n, kt, h) for kt in kts for h in ((0,) if kt == "B" else (0, 1))] or [None]
                a2, n2 = divmod(c + 2, NG)
                units = s_units(a2) if 0 <= c + 2 < ROUNDS else []
                weight = [step_columns(step) for step in st]
                cost = [unit_columns(a2, u) for u in units]
                starts = [sum(cost[0:i]) / max(sum(cost), 1) for i in range(len(units))]
                ends = [sum(weight[0:i + 1]) / sum(weight) for i in range(len(st))]
                for i, step in enumerate(st):
                    part = [u for u, x0 in zip(units, starts) if x0 < ends[i] and (i == 0 or x0 >= ends[i - 1])]
                    values = None
                    if step and (step[3] == 1 or step[2] == "B") and step[2] != kts[0]:
                        values = (a, n, kts[kts.index(step[2]) - 1])
                    if i == 0 and 0 < c <= ROUNDS:
                        a1, n1 = divmod(c - 1, NG)
                        values = (a1, n1, KEY_TILES[a1][-1])
                    STEPS.append({"round": c, "take_acc": i == min(1, len(st) - 1) and 0 < c <= ROUNDS, "step": step,
                                  "units": (a2, n2, part) if part else None, "values": values, "jobs": [],
                                  "length": STEP_LENGTH[a] if step else 4.0})

        plan_rounds()

        def at(c, i):
            same = [k for k, s in enumerate(STEPS) if s["round"] == c]
            return same[min(i, len(same) - 1)]

        HIDDEN = ("hid", "gate", "lin")

        def takes_hidden(s):
            return not (s["step"] and s["step"][3] == 0) and not any(job[0] in HIDDEN for job in s["jobs"])

        def chain(start, jobs, scale=1.0):
            k, spent = start, 0.0
            for wait, job in jobs:
                while spent < wait * scale or (job[0] in HIDDEN and not takes_hidden(STEPS[k])):
                    spent += STEPS[k]["length"]
                    k += 1
                    if k == len(STEPS):
                        STEPS.append({"round": ROUNDS + 1, "take_acc": False, "step": None,
                                      "units": None, "values": None, "jobs": [], "length": LAST_LENGTH})
                spent = 0.0
                STEPS[k]["jobs"].insert(0 if job[0] in HIDDEN else len(STEPS[k]["jobs"]), job)
            return k


        def norm(k, b):
            return [(1.2, ("stats", k, b)), (2.4, ("hat", k, b))]

        def place_split(k, job):
            chain(k, [(0, job), (MID_WAIT, ("mid", *job))])

        def plan_jobs():
            ready = {(CAUSAL, 0): 0}
            STEPS[0]["jobs"] += [("q", CAUSAL, 0), ("k", CAUSAL, 0), ("rest", 0),
                                 ("mid", "q", CAUSAL, 0), ("mid", "k", CAUSAL, 0), ("kc", 0),
                                 ("mid", "kc", 0), ("v", CAUSAL, 0), ("stats", 0, 1), ("vc", 0),
                                 ("hat", 0, 1), ("turn", 0, 1)]
            ready[(CAUSAL, 1)] = 0
            for b in range(2, B):
                ready[(CAUSAL, b)] = chain(at(4 * b - 9, 0), norm(0, b) + [(1.2, ("turn", 0, b))])
            for i in range(3 * B):
                a, b = divmod(i, B)
                k = at(4 * i - 6, Q_STEP) if i else 0
                if (a, b) != (CAUSAL, 0):
                    k = max(k, ready[(a, b)] + 1)
                    assert STEPS[k]["round"] <= 4 * i - 5
                if i:
                    place_split(k, ("q", a, b))
                if a != CROSS and i:
                    k = max(k, at(4 * i - 5, K_STEP))
                    assert STEPS[k]["round"] <= 4 * i - 4
                    place_split(k, ("k", a, b))
                    STEPS[max(k, at(4 * i - 4, V_STEP))]["jobs"].append(("v", a, b))
                for g in range(GROUPS):
                    c = 4 * i + g
                    STEPS[at(c - 1, NM_STEP)]["jobs"].append(("nm", a, c % NG))
                    STEPS[at(c + 1, OUT_STEP)]["jobs"].append(("out", a, c % NG))
                k = at(4 * i + 4, OUT_STEP)
                if a == CAUSAL:
                    ready[(SELF, b)] = chain(k, norm(1, b) + norm(2, b) + [
                        (0.1, ("bias", "b2", b)), (1.2, ("turn", 2, b)), (1.2, ("hid", b)),
                        (2.5, ("ffn", CAUSAL, b)), (0.1, ("bias", "bo1", b))] + norm(3, b)
                        + [(1.2, ("turn", 3, b))], CHAIN_SCALE[a])
                elif a == SELF:
                    ready[(CROSS, b)] = chain(k, [(1.2, ("turn", 11, b)), (1.2, ("wo", SELF, b)),
                                                  (0.1, ("bias", "bo2", b))] + norm(4, b)
                                              + [(1.2, ("turn", 4, b))], CHAIN_SCALE[a])
                else:
                    chain(max(k, at(*TAIL_START[b])), [(1.2, ("turn", 12, b)), (1.2, ("wo", CROSS, b)),
                                                         (0.1, ("bias", "bff2", b))]
                          + norm(5, b) + [(1.2, ("turn", 5, b)), (1.2, ("gate", b)), (3.5, ("lin", b)),
                                          (3.0, ("ffn", CROSS, b)), (1.2, ("bias", "m", b)),
                                          (0.1, ("turn", 7, b)), (1.2, ("qd", "m", b)), (1.0, ("kd", b)),
                                          (1.0, ("vd", b)), (0.1, ("Sd", "m", b)), (1.2, ("kx", "c", b)),
                                          (1.0, ("vx", "c", b)), (1.2, ("pt", "m", b)), (2.0, ("pv", "m", b))]
                          + norm(6, b) + norm(7, b)
                          + [(0.1, ("bias", "c", b)), (1.2, ("turn", 8, b)), (1.2, ("qd", "c", b)),
                             (1.2, ("Sd", "c", b)), (1.2, ("kx", "d", b)), (1.0, ("vx", "d", b)),
                             (0.1, ("pt", "c", b)), (1.2, ("pv", "c", b))]
                          + norm(8, b) + norm(9, b)
                          + [(1.2, ("turn", 9, b)), (1.2, ("h1", b)), (1.2, ("h2", b)),
                             (1.2, ("stats", 10, b)), (2.4, ("hat", 10, b)), (1.2, ("turn", 10, b)),
                             (1.2, ("qd", "d", b)), (1.2, ("Sd", "d", b)), (2.4, ("pt", "d", b)),
                             (1.2, ("pv", "d", b))], TAIL_SCALE[b])
            place_split(at(2, 0), ("kc", 1))
            chain(at(2, 0), [(1.5, ("vc", 1))])

        plan_jobs()
        nth, seen = {}, {}
        for s in STEPS:
            if s["step"] and s["step"][3] == 0:
                a, n, kt, _ = s["step"]
                last = kt == KEY_TILES[a][-1]
                add_slot((a, n, kt), ("acc", a, n) if last else None)
                if not last:
                    reads[len(slot_reader) - 1] = len(reads) + 1
                if a == CAUSAL and kt not in ("A", "B"):
                    mask_no[(a, n, kt)] = len(mask_no) + 1
            for job in s["jobs"]:
                seen[job[0]] = seen.get(job[0], 0) + 1
                nth[job] = seen[job[0]]
                if job[0] == "hid":
                    add_slot(("ffn", CAUSAL, job[1]), ("ffn", CAUSAL, job[1]))
                elif job[0] == "lin":
                    add_slot(("ffn", CROSS, job[1]), ("ffn", CROSS, job[1]))
                elif job[0] == "pt":
                    add_slot(("PT", *job[1:]), ("pv", *job[1:]))
        max_no = {}
        for s in STEPS:
            for job in s["jobs"]:
                if job[0] == "Sd":
                    for half in range(2 if job[1] == "m" else 1):
                        max_no[(*job, half)] = len(max_no) + 1
        OPERANDS = [job for s in STEPS for job in s["jobs"] if job[0] in ("q", "k", "kc")]
        op_no = {k: i for i, k in enumerate(OPERANDS)}
        NORM_ORDER = {k: [job[2] for s in STEPS for job in s["jobs"] if job[0] == "stats" and job[1] == k]
                      for k in range(NORMS)}
        assert all(v == sorted(v) for v in NORM_ORDER.values())

        def load_weight(eng, name):
            src = inp[name]
            n = [m for m, _ in WEIGHTS].index(name)
            dst = w[name][:, :]
            if src.shape[0] > P:
                src = src.rearrange("(c p) d -> p c d", p=P)
                dst = dst.rearrange("p (c d) -> p c d", d=D)
            eng.dma_start(dst, src).then_inc(w_loaded[sum(n >= k for k in WEIGHT_SETS[1:])], 16)

        def load_broadcast(eng, i):
            name, o = BROADCASTS[i]
            eng.dma_start(bc[:, i, :], inp[name][o:o + D].partition_broadcast(P))\
               .then_inc(bc_loaded[int(i >= BROADCAST_SETS[1])], 16)

        block = ctx.enter_context(nc.Block())

        def next_unit(s):
            units = ("MISC", "S0", "S1") if s["round"] <= ROUNDS else ("MISC", "S0", "S1", "ACC")
            turns.append(0)
            return units[len(turns) % len(units)]

        turns = []

        def pe_columns(pe, i):
            pe.wait_ge(rows_loaded[i], 16 * (len(COLUMNS) - FIRST_COLUMNS if i else FIRST_COLUMNS))
            ps = claim(pe, "S0", ("col", i))
            n = rows[i].shape[0]
            pe.transpose(ps[:, 0:n], rows[i][:, :], ident[0:n, 0:n]).then_inc(filled["S0"], 1)

        def pe_context_turned(pe):
            pe.wait_ge(ctx_loaded, 32)
            for key, u, src, n in (("ctxA", "S1", ctx_a, P), ("ctxB", "MISC", ctx_b, SB)):
                ps = claim(pe, u, key)
                for b in range(B):
                    mm = pe.transpose(ps[:, b * n:(b + 1) * n], src[:, b, :], ident[0:n, 0:n])
                mm.then_inc(filled[u], 1)

        def pe_setup(pe):
            pe.wait_ge(consts, 6)
            pe_columns(pe, 0)
            pe_turn(pe, 0, 0, tm, "ACC")
            pe.wait_ge(w_loaded[0], 16 * WEIGHT_SETS[1])

        CONTEXT = ("L0_xattn_w_ckv", "L1_xattn_Wkv2")

        def pe_context_keys(pe, i):
            if i == 0:
                await_taken(pe, "ctxA")
                await_taken(pe, "ctxB")
            ps = claim(pe, "AB"[i], ("kc", i))
            wk = w[CONTEXT[i]][:, 0:D]
            pe.matmul(ps[:, 0:T], wk, ctx_t[:, 0:T], start=True, stop=True)
            pe.matmul(ps[:, T:B * S], wk, ctx_t[:, T:B * S], start=True, stop=True)\
              .then_inc(filled["AB"[i]], 1)

        def pe_context_values(pe, i):
            wv = w[CONTEXT[i]][:, D:2 * D]
            ps = claim(pe, "A", ("vc", i))
            for b in range(B):
                pe.matmul(ps[:, b * D:(b + 1) * D], ctx_t[:, b * S:b * S + P], wv, start=True, stop=True)
            for b in range(B):
                for j in range(4):
                    mm = pe.matmul(ps[KB * j:KB * j + KB, T + b * D:T + (b + 1) * D],
                                   ctx_t[:, (b + 1) * S - KB:(b + 1) * S], wv,
                                   start=True, stop=True, tile_position=(0, 32 * j))
            mm.then_inc(filled["A"], 1)

        def pe_turn(pe, k, b, src, u):
            if k in (0, 2, 3, 4, 5):
                pe.wait_ge(hat_ready[k], b + 1)
            elif k in (11, 12):
                await_taken(pe, ("out", SELF if k == 11 else CROSS, GROUPS * b + GROUPS - 1))
            else:
                await_x(pe, {7: "bff2", 8: "m", 9: "c", 10: "f"}[k], b)
            ps = claim(pe, u, ("turn", k, b))
            for t in range(NT):
                mm = pe.transpose(ps[:, t * P:(t + 1) * P], src[:, NT * b + t, :], ident[:, :])
            mm.then_inc(filled[u], 1)

        PROJ = {CAUSAL: (0, ("L0_xattn_w_qkv", 0), ("L0_xattn_w_qkv", D), ("L0_xattn_w_qkv", 2 * D)),
                SELF: (3, ("L1_xattn_Wq1", 0), ("L1_xattn_Wkv1", 0), ("L1_xattn_Wkv1", D)),
                CROSS: (4, ("L1_xattn_Wq2", 0), None, None)}

        def pe_project(pe, a, b, what, u):
            await_taken(pe, ("turn", PROJ[a][0], b))
            name, o = PROJ[a][1 + "qkv".index(what)]
            ps = claim(pe, u, (what, a, b))
            if what == "v":
                for t in range(NT):
                    mm = pe.matmul(ps[:, t * D:(t + 1) * D], fm[:, b, t * P:(t + 1) * P],
                                   w[name][:, o:o + D], start=True, stop=True)
            else:
                mm = pe.matmul(ps[:, :], w[name][:, o:o + D], fm[:, b, :], start=True, stop=True)
            mm.then_inc(filled[u], 1)

        def pe_scores_for_max(pe, s, a, n, units):
            b, g = divmod(n, GROUPS)
            l = 0 if a == CAUSAL else 1
            c = NG * a + n
            if units[0] == s_units(a)[0]:
                pe.wait_ge(q_stacked[c % QR], STACKED * (c // QR + 1))
            if g == 0 and units[0] == s_units(a)[0]:
                if a != CROSS:
                    pe.wait_ge(k_stacked[b % 2], STACKED * ((B * a + b) // 2 + 1))
            for j, what, i in units:
                h = 4 * g + j
                pair = h // 2
                u = next_unit(s)
                ps = claim(pe, u, ("S", a, n, j, what, i))
                q = q_stack[0:NEG, c % QR, j, :]
                if what == "self":
                    m = keys_seen(a, i)
                    pe.matmul(ps[:, 0:m], q[:, i * P:(i + 1) * P],
                              k_stack[0:NEG, b % 2, pair, 0:m],
                              start=True, stop=True).then_inc(filled[u], 1)
                else:
                    if n == 0:
                        pe.wait_ge(kc_stacked[l], STACKED)
                    for qt in (i, i + 1):
                        mm = pe.matmul(ps[:, (qt - i) * S:(qt - i + 1) * S], q[:, qt * P:(qt + 1) * P],
                                       kc_stack[0:NEG, l, pair, b * S:(b + 1) * S],
                                       start=True, stop=True)
                    mm.then_inc(filled[u], 1)

        def pe_turn_max(pe, a, n, u):
            c = NG * a + n
            pe.wait_ge(nm_ready, c + 1)
            ps = claim(pe, u, ("nm", a, n))
            for t in range(NT):
                mm = pe.transpose(ps[0:8, t * P // 2:(t + 1) * P // 2].bitcast(BF16),
                                  nm[:, c % 2, t, :, :].rearrange("p k j -> p (k j)"), identb[:, :])
            mm.then_inc(filled[u], 1)

        def pe_shifted_scores(pe, a, n, kt, half):
            b, g = divmod(n, GROUPS)
            c = NG * a + n
            l = 0 if a == CAUSAL else 1
            if kt == KEY_TILES[a][0] and half == 0:
                pe.wait_ge(neg_rows[c % 2], NEG_ROWS * (c // 2 + 1))
            u = "AB"[half]
            ps = claim(pe, u, ("ST", a, n, kt, half))
            q0 = first_query(a, kt)
            for j in (range(4) if kt == "B" else (2 * half, 2 * half + 1)):
                h = 4 * g + j
                pair, at = h // 2, (j % 2) * T
                q = q_stack[:, c % QR, j, q0:T]
                if kt == "B":
                    mm = pe.matmul(ps[KB * j:KB * j + KB, 0:T], kc_stack[:, l, pair, (b + 1) * S - KB:(b + 1) * S], q,
                                   start=True, stop=True, tile_position=(0, 32 * j))
                else:
                    k = (kc_stack[:, l, pair, b * S:b * S + P] if kt == "A"
                         else k_stack[:, b % 2, pair, kt * P:(kt + 1) * P])
                    mm = pe.matmul(ps[:, at:at + T - q0], k, q, start=True, stop=True)
            mm.then_inc(filled[u], 1)

        def pe_weighted_values(pe, a, n, kt):
            b, g = divmod(n, GROUPS)
            l = 0 if a == CAUSAL else 1
            e = slot((a, n, kt))
            first, last = kt == KEY_TILES[a][0], kt == KEY_TILES[a][-1]
            if first:
                claim(pe, "ACC", ("acc", a, n))
                if a != CROSS and g == 0:
                    await_taken(pe, ("v", a, b))
                if n == 0 and a != SELF:
                    pe.wait_ge(once_only, 4 * (l + 1))
            for half in ((0,) if kt == "B" else (0, 1)):
                await_taken(pe, ("ST", a, n, kt, half))
            if (a, n, kt) in mask_no:
                pe.wait_ge(mask_done, mask_no[(a, n, kt)])
            ps = bank("ACC")
            q0 = first_query(a, kt)
            for j in range(4):
                h = 4 * g + j
                o = ps[32 * j:32 * j + DH + 1, q0:T]
                if kt == "B":
                    rr = slice(KB * j, KB * j + KB)
                    mm = pe.matmul(o, vc_b[rr, l, b, g, :], e[rr, 0, :], start=first, stop=last,
                                   tile_position=(32 * j, 32 * j), skip_group_check=True)
                else:
                    v = vc_a[:, l, b, h, :] if kt == "A" else v_self[:, b % 2, kt, h, :]
                    mm = pe.matmul(o, v, e[:, j, 0:T - q0], start=first, stop=last,
                                   tile_position=(0, 32 * j), skip_group_check=True)
            mm.then_inc(filled["ACC"] if last else slot_read, 1)

        def pe_turn_out(pe, a, n, u):
            await_taken(pe, ("acc", a, n))
            ps = claim(pe, u, ("out", a, n))
            for t in range(NT):
                mm = pe.transpose(ps[:, t * P:(t + 1) * P],
                                  acc_s[:, (NG * a + n) % 2, t * P:(t + 1) * P], ident[:, :])
            mm.then_inc(filled[u], 1)

        def pe_token_major(pe, key, src, name, u):
            ps = claim(pe, u, key)
            for t in range(NT):
                mm = pe.matmul(ps[:, t * D:(t + 1) * D], src[:, t * P:(t + 1) * P], w[name][:, :],
                               start=True, stop=True)
            mm.then_inc(filled[u], 1)

        def pe_hidden(pe, job, c):
            what, b = job
            k, name = (2, "L0_xattn_w1") if what == "hid" else (5, "L1_xattn_Wff1")
            first = 2 * c + (FC if what == "gate" else 0)
            await_taken(pe, ("turn", k, b))
            if job == ("hid", 0):
                pe.wait_ge(w_loaded[1], 16 * (WEIGHT_SETS[2] - WEIGHT_SETS[1]))
            u = "AB"[c]
            ps = claim(pe, u, (*job, c))
            for i in range(2):
                mm = pe.matmul(ps[:, i * T:(i + 1) * T], w[name][:, (first + i) * P:(first + i + 1) * P],
                               fm[:, b, :], start=True, stop=True)
            mm.then_inc(filled[u], 1)

        def pe_ffn_out(pe, a, b, u):
            name = "L0_xattn_w2" if a == CAUSAL else "L1_xattn_Wff2"
            for c in range(2):
                await_taken(pe, ("hid" if a == CAUSAL else "lin", b, c))
            ps = claim(pe, u, ("ffn", a, b))
            hid = slot(("ffn", a, b))
            for t in range(NT):
                for c in range(FC):
                    mm = pe.matmul(ps[:, t * D:(t + 1) * D], hid[:, c, t * P:(t + 1) * P],
                                   w[name][:, c * D:(c + 1) * D], start=(c == 0), stop=(c == FC - 1))
            mm.then_inc(filled[u], 1)

        ONE_HEAD = {"m": (7, "L2_xattn_wq_m"), "c": (8, "L2_xattn_wq_c"), "d": (10, "L3_xattn_Wq")}
        CONTEXT_1 = {"c": ("L2_xattn_wk_c", "L2_xattn_wv_c"), "d": ("L3_xattn_Wk", "L3_xattn_Wv")}

        def queries(b):
            return tail[b][:, 0:T]

        def keys(a, b):
            o = {"m": T, "c": 1540, "d": T}[a]
            return tail[b][:, o:o + KEYS[a]]

        def values_1(a, b, kt):
            if a == "m":
                return tail[b][:, 2 * T:3 * T]
            o = {"c": 1540, "d": T}[a] + S + kt * D
            return tail[b][0:(P, SB)[kt], o:o + D]

        def probs(a, b):
            if a == "m":
                return probs_m[b]
            return tail[b][:, 924:924 + NT * S].rearrange("p (t k) -> p t k", t=NT)

        def pe_feature_major(pe, key, wk, src, u):
            ps = claim(pe, u, key)
            pe.matmul(ps[:, 0:src.shape[-1]], wk, src, start=True, stop=True).then_inc(filled[u], 1)

        def pe_context_values_1(pe, a, b, u):
            ps = claim(pe, u, ("vx", a, b))
            wv = w[CONTEXT_1[a][1]][:, :]
            pe.matmul(ps[:, 0:D], ctx_t[:, b * S:b * S + P], wv, start=True, stop=True)
            pe.matmul(ps[0:SB, D:2 * D], ctx_t[:, b * S + P:(b + 1) * S], wv, start=True, stop=True)\
              .then_inc(filled[u], 1)

        def sd_units(a, b):
            if a == "m":
                return [(("Sd", a, b, half), "AB"[half], (2 * half, 2 * half + 1)) for half in range(2)]
            return [(("Sd", a, b, 0), "AB"[b % 2], (0, 1, 2, 3))]

        def sd_tile(ps, a, i):
            o = i * (T if a == "m" else T // 2)
            return ps[:, o:o + KEYS[a]]

        def pe_one_head_scores(pe, a, b):
            await_taken(pe, ("qd", a, b))
            await_taken(pe, ("kd", b) if a == "m" else ("kx", a, b))
            for key, u, ts in sd_units(a, b):
                ps = claim(pe, u, key)
                for i, t in enumerate(ts):
                    mm = pe.matmul(sd_tile(ps, a, i), queries(b)[:, t * P:(t + 1) * P], keys(a, b),
                                   start=True, stop=True)
                mm.then_inc(filled[u], 1)

        def pe_turn_probs(pe, s, a, b):
            e = probs(a, b)
            for key, _, _ in sd_units(a, b):
                await_taken(pe, key)
            if a == "m":
                for half in range(2):
                    u = "AB"[half]
                    ps = claim(pe, u, ("pt", a, b, half))
                    for i in range(2):
                        for kt in range(NT):
                            mm = pe.transpose(ps[:, i * T + kt * P:i * T + (kt + 1) * P],
                                              e[:, 2 * half + i, kt * P:(kt + 1) * P], ident[:, :])
                    mm.then_inc(filled[u], 1)
            else:
                for i, (k0, m) in enumerate(((0, P), (P, SB))):
                    u = next_unit(s)
                    ps = claim(pe, u, ("pt", a, b, i))
                    for t in range(NT):
                        mm = pe.transpose(ps[0:m, t * P:(t + 1) * P], e[:, t, k0:k0 + m], ident[:, :])
                    mm.then_inc(filled[u], 1)

        def pe_one_head_values(pe, a, b, u):
            pt = slot(("PT", a, b))
            for i in range(2):
                await_taken(pe, ("pt", a, b, i))
            await_taken(pe, ("vd", b) if a == "m" else ("vx", a, b))
            ps = claim(pe, u, ("pv", a, b))
            for t in range(NT):
                o = ps[:, t * D:(t + 1) * D]
                if a == "m":
                    v = values_1(a, b, 0)
                    for kt in range(NT):
                        mm = pe.matmul(o, pt[:, t, kt * P:(kt + 1) * P], v[:, kt * D:(kt + 1) * D],
                                       start=(kt == 0), stop=(kt == NT - 1))
                else:
                    pe.matmul(o, pt[:, 0, t * P:(t + 1) * P], values_1(a, b, 0), start=True, stop=False)
                    mm = pe.matmul(o, pt[0:SB, 1, t * P:(t + 1) * P], values_1(a, b, 1),
                                   start=False, stop=True)
            mm.then_inc(filled[u], 1)

        def pe_job(pe, s, job):
            what, a, b = (*job, None)[0:3]
            if what == "nm":
                pe_turn_max(pe, a, b, next_unit(s))
            elif what == "out":
                pe_turn_out(pe, a, b, next_unit(s))
            elif what == "rest":
                pe_columns(pe, 1)
                pe_context_turned(pe)
            elif what in ("q", "k", "v"):
                pe_project(pe, a, b, what, next_unit(s))
            elif what == "kc":
                if a == 1:
                    pe.wait_ge(w_loaded[1], 16 * (WEIGHT_SETS[2] - WEIGHT_SETS[1]))
                pe_context_keys(pe, a)
            elif what == "vc":
                pe_context_values(pe, a)
            elif what == "turn":
                pe_turn(pe, a, b, x if a in (7, 8, 9, 10) else tm, next_unit(s))
            elif what == "ffn":
                pe_ffn_out(pe, a, b, next_unit(s))
            elif what == "wo":
                await_taken(pe, ("turn", 11 if a == SELF else 12, b))
                pe_token_major(pe, job, fm[:, b, :], "L1_xattn_Wo1" if a == SELF else "L1_xattn_Wo2",
                               next_unit(s))
            elif what == "qd":
                k, wq = ONE_HEAD[a]
                if job == ("qd", "m", 0):
                    pe.wait_ge(w_loaded[2], 16 * (WEIGHT_SETS[3] - WEIGHT_SETS[2]))
                await_taken(pe, ("turn", k, b))
                pe_feature_major(pe, job, w[wq][:, :], fm[:, b, :], next_unit(s))
            elif what == "kd":
                pe_feature_major(pe, job, w["L2_xattn_wk_m"][:, :], fm[:, a, :], next_unit(s))
            elif what == "vd":
                pe_token_major(pe, job, fm[:, a, :], "L2_xattn_wv_m", next_unit(s))
            elif what == "kx":
                pe_feature_major(pe, job, w[CONTEXT_1[a][0]][:, :], ctx_t[:, b * S:(b + 1) * S], next_unit(s))
            elif what == "vx":
                pe_context_values_1(pe, a, b, next_unit(s))
            elif what == "Sd":
                pe_one_head_scores(pe, a, b)
            elif what == "pt":
                pe_turn_probs(pe, s, a, b)
            elif what == "pv":
                pe_one_head_values(pe, a, b, next_unit(s))
            elif what == "h1":
                await_taken(pe, ("turn", 9, a))
                pe_feature_major(pe, job, w["L2_xattn_f0_w"][:, :], fm[:, a, :], next_unit(s))
            elif what == "h2":
                await_taken(pe, ("h1", a))
                pe_token_major(pe, job, queries(a), "L2_xattn_f1_w", next_unit(s))

        @block.tensor
        def _(pe):
            pe_setup(pe)
            for s in STEPS:
                if s["step"]:
                    pe_shifted_scores(pe, *s["step"])
                hidden = [job for job in s["jobs"] if job[0] in HIDDEN]
                for job in hidden:
                    pe_hidden(pe, job, 0)
                if s["units"]:
                    pe_scores_for_max(pe, s, *s["units"])
                for job in hidden:
                    pe_hidden(pe, job, 1)
                if s["values"]:
                    pe_weighted_values(pe, *s["values"])
                for job in s["jobs"]:
                    pe_job(pe, s, job)

        IDN = ACT.Identity

        def act_raw(act, key, scale, bias):
            o = op_no[key]
            ps = await_bank(act, key)
            m = B * S if key[0] == "kc" else T
            if o >= 2:
                act.wait_ge(bounced[o % 2], BOUNCED * (o // 2))
            act.activation(raw[:, o % 2, 0:m], ps[:, 0:m], IDN, bias=bias, scale=scale)
            act.activation(parts[:, o % 2, 0, 0:m], ps[:, 0:m], IDN, bias=bias, scale=scale)\
               .then_inc(frees(key), 1)

        def act_project(act, a, b, what):
            if what == "q":
                bias = colx[:, 0:1] if a == CAUSAL else 0.0
                act_raw(act, ("q", a, b), HEAD_SCALE[a], bias)
            elif what == "k":
                act_raw(act, ("k", a, b), 1.0, colv("L0_xattn_b_qkv", 1) if a == CAUSAL else 0.0)

        def act_setup(act):
            act_columns(act, 0)
            await_taken(act, ("col", 0))
            act_turn(act, 0, 0)
            act.wait_ge(colx_ready, 1)

        def act_columns(act, i):
            ps = await_bank(act, ("col", i))
            c = slice(0, FIRST_ROWS) if i == 0 else slice(FIRST_ROWS, ALL_ROWS)
            act.copy(col[:, c], ps[:, 0:c.stop - c.start]).then_inc(frees(("col", i)), 1)

        def act_rest_of_setup(act):
            act_columns(act, 1)
            ct = ctx_t[:, :].rearrange("p (b s) -> p b s", s=S)
            for key, k0, m in (("ctxA", 0, P), ("ctxB", P, SB)):
                ps = await_bank(act, key)
                act.copy(ct[:, :, k0:k0 + m], ps[:, 0:B * m].rearrange("p (b s) -> p b s", s=m))\
                   .then_inc(frees(key), 1)

        GAINS = {0: ("L0_xattn_g1", "L0_xattn_be1"), 2: ("L0_xattn_gf", "L0_xattn_bf"),
                 3: ("L1_xattn_ln1_s", "L1_xattn_ln1_b"), 4: ("L1_xattn_ln2_s", "L1_xattn_ln2_b"),
                 5: ("L1_xattn_ln3_s", "L1_xattn_ln3_b")}

        def act_turn(act, k, b):
            key = ("turn", k, b)
            ps = await_bank(act, key)
            if k in GAINS:
                gain, plus = GAINS[k]
                act.activation(fm[:, b, :], ps[:, :], IDN, bias=colv(plus), scale=colv(gain))\
                   .then_inc(frees(key), 1)
            else:
                act.copy(fm[:, b, :], ps[:, :]).then_inc(frees(key), 1)

        def act_exp(act, a, n, kt, half):
            key = ("ST", a, n, kt, half)
            ps = await_bank(act, key)
            e = slot((a, n, kt))
            if half == 0:
                await_slot(act, (a, n, kt))
            m = T - first_query(a, kt)
            if kt == "B":
                ex = act.activation(e[:, 0, :], ps[:, 0:T], ACT.Exp)
            else:
                pv = ps.rearrange("p (j t) -> p j t", j=2)
                ex = act.activation(e[:, 2 * half:2 * half + 2, 0:m], pv[:, :, 0:m], ACT.Exp)
            ex.then_inc(frees(key), 1)

        def act_job(act, job):
            what, a, b = (*job, None)[0:3]
            if what == "nm":
                ps = await_bank(act, job)
                act.copy(nmt[:, (NG * a + b) % 2, :], ps[0:8, 0:T // 2].bitcast(BF16))\
                   .then_inc(frees(job), 1)
            elif what == "rest":
                act_rest_of_setup(act)
            elif what in ("q", "k"):
                act_project(act, a, b, what)
            elif what == "kc":
                act_raw(act, job, 1.0, 0.0 if a else colv("L0_xattn_b_ckv"))
            elif what == "turn":
                if job == ("turn", 0, 1):
                    await_taken(act, ("col", 1))
                    act.wait_ge(colx_ready, 4)
                act_turn(act, a, b)
            elif what == "hid":
                await_slot(act, ("ffn", CAUSAL, a))
                hid = slot(("ffn", CAUSAL, a))
                for c in range(2):
                    ps = await_bank(act, (*job, c))
                    for i in range(2):
                        m = 2 * c + i
                        g = act.activation(hid[:, m, :], ps[:, i * T:(i + 1) * T], ACT.Gelu,
                                           bias=colv("L0_xattn_b1", m))
                    g.then_inc(frees((*job, c)), 1)
            elif what == "gate":
                for c in range(2):
                    ps = await_bank(act, (*job, c))
                    for i in range(2):
                        m = 2 * c + i
                        act.activation(tail[a][:, m * T:(m + 1) * T], ps[:, i * T:(i + 1) * T], ACT.Sigmoid,
                                       bias=colx[:, 3 + m:4 + m], scale=1.702).then_inc(sig_ready, 1)
            elif what == "qd":
                ps = await_bank(act, job)
                act.activation(queries(b), ps, IDN,
                               bias=0.0 if a == "d" else colx[:, 1 + "mc".index(a):2 + "mc".index(a)],
                               scale=float(D) ** -0.5 if a == "d" else 0.125).then_inc(frees(job), 1)
            elif what == "kd":
                ps = await_bank(act, job)
                act.activation(keys("m", a), ps, IDN, bias=colv("L2_xattn_bk_m")).then_inc(frees(job), 1)
            elif what == "kx":
                if a == "d":
                    await_bank(act, ("Sd", "m", b, 1))
                ps = await_bank(act, job)
                act.activation(keys(a, b), ps[:, 0:S], IDN, bias=colv("L2_xattn_bk_c") if a == "c" else 0.0)\
                   .then_inc(frees(job), 1)
            elif what == "Sd":
                if a == "m" and b > 0:
                    await_bank(act, ("ST", CROSS, NG - 1, "B", 0))
                for key, _, ts in sd_units(a, b):
                    act.wait_ge(dmaxed, max_no[key])
                    ps = await_bank(act, key)
                    for i, t in enumerate(ts):
                        ex = act.activation(probs(a, b)[:, t, 0:KEYS[a]], sd_tile(ps, a, i), ACT.Exp,
                                            bias=nmx[:, b, t:t + 1], accum_out=rsum[:, b, t:t + 1])
                    ex.then_inc(frees(key), 1)
            elif what == "pt":
                await_slot(act, ("PT", a, b))
                pt = slot(("PT", a, b))
                for i, m in enumerate((P, P) if a == "m" else (P, SB)):
                    ps = await_bank(act, (*job, i))
                    if a == "m":
                        r = act.copy(pt[:, 2 * i:2 * i + 2, :], ps.rearrange("p (i t) -> p i t", i=2))
                    else:
                        r = act.copy(pt[0:m, i, :], ps[0:m, :])
                    r.then_inc(frees((*job, i)), 1)
            elif what == "h1":
                ps = await_bank(act, job)
                act.activation(queries(a), ps, ACT.Gelu, bias=colv("L2_xattn_f0_b")).then_inc(frees(job), 1)
            elif what == "h2":
                await_taken(act, job)
                act.activation(tiles(tm, a), tiles(tm, a), ACT.Gelu).then_inc(h2_ready, 1)

        @block.scalar
        def _(act):
            for name, _ in WEIGHTS[0:2]:
                load_weight(act, name)
            for i in range(BROADCAST_SETS[1]):
                load_broadcast(act, i)
            act_setup(act)
            for s in STEPS:
                if s["step"]:
                    act_exp(act, *s["step"])
                if s["take_acc"]:
                    a, n = divmod(s["round"] - 1, NG)
                    ps = await_bank(act, ("acc", a, n))
                    act.copy(acc_s[:, (NG * a + n) % 2, :], ps).then_inc(frees(("acc", a, n)), 1)
                for job in s["jobs"]:
                    act_job(act, job)

        def dve_stats(dve, k, b, src):
            for t in range(NT):
                i = dve.bn_stats(st[:, b, t, :], src[:, NT * b + t, :])
            i.then_inc(stats_done[k], 1)
            dve.wait_ge(stats_done[k], b + 1)
            for t in range(NT):
                i = dve.bn_aggr(mv[:, b, t, :], st[:, b, t, :])
            i.then_inc(moments[k], 1)

        def dve_affine(dve, k, b):
            key, dst, gain, plus = AFFINE[k]
            dve.wait_ge(hat_ready[k], b + 1)
            if plus is None:
                dve.wait_ge(x_biased[key[0]], b + 1)
            for t in range(NT):
                i = dve.scalar_tensor_tensor(out=dst[:, NT * b + t, :], in0=tm[:, NT * b + t, :],
                                             scalar=rs[:, b, t:t + 1],
                                             in1=xb[:, NT * b + t, :] if plus is None else bcv(plus),
                                             op0=ALU.mult, op1=ALU.add)
            i.then_inc(affined[key], 1)

        def dve_hat(dve, k, b, src):
            dve.wait_ge(rstd_ready[k], b + 1)
            if k in AFFINE:
                key, dst, gain, plus = AFFINE[k]
                for t in range(NT):
                    i = dve.scalar_tensor_tensor(out=tm[:, NT * b + t, :], in0=src[:, NT * b + t, :],
                                                 scalar=mv[:, b, t, 0:1], in1=bcv(gain),
                                                 op0=ALU.subtract, op1=ALU.mult)
                i.then_inc(hat_ready[k], 1)
                dve_affine(dve, k, b)
                return
            for t in range(NT):
                i = dve.tensor_scalar(tm[:, NT * b + t, :], src[:, NT * b + t, :], mv[:, b, t, 0:1],
                                      rs[:, b, t:t + 1], ALU.subtract, ALU.mult)
            i.then_inc(hat_ready[k], 1)

        def dve_scores_max(dve, a, n, units):
            b, g = divmod(n, GROUPS)
            c = (NG * a + n) % 2
            for j, what, i in units:
                key = ("S", a, n, j, what, i)
                ps = await_bank(dve, key)
                if what == "ctx":
                    r = dve.tensor_reduce(mxc[:, c, i:i + 2, j], ps[:, 0:2 * S].rearrange("p (t s) -> p t s", s=S),
                                          AX.X, ALU.max)
                elif a == CAUSAL:
                    m = keys_seen(a, i)
                    masked = junk[:, ("MISC", "S0", "S1").index(turn[key][0]), 0:m]
                    r = dve.tensor_tensor_reduce(masked, ps[:, 0:m], mask[:, T - m:T], 1.0, LOWEST,
                                                 ALU.add, ALU.max, mx[:, c, i, j:j + 1])
                else:
                    r = dve.tensor_reduce(mx[:, c, i, j:j + 1], ps, AX.X, ALU.max)
                r.then_inc(frees(key), 1)
            if a == CAUSAL and units and units[-1] == s_units(a)[-1]:
                for j in (2, 3):
                    await_taken(dve, ("S", a, n, j, "ctx", 2))
                dve.tensor_tensor(mx[:, c, :, :], mx[:, c, :, :], mxc[:, c, :, :], ALU.max).then_inc(max_joined, 1)

        def dve_out(dve, a, n):
            b, g = divmod(n, GROUPS)
            c = NG * a + n
            key = ("out", a, n)
            ps = await_bank(dve, key).rearrange("p (t j e) -> p t j e", t=NT, e=32)
            dve.reciprocal(rden[:, c % 2, :, :], ps[:, :, :, DH]).then_inc(rden_ready, 1)
            dve.wait_ge(rden_ready, c + 1)
            o = tiles(tm, b)[:, :, 32 * g:32 * g + 32].rearrange("p t (j d) -> p t j d", d=DH)
            dve.tensor_tensor(o, ps[:, :, :, 0:DH],
                              rden[:, c % 2, :, :].unsqueeze(3).to_broadcast([P, NT, 4, DH]), ALU.mult)\
               .then_inc(frees(key), 1)
            if a == CAUSAL and g == GROUPS - 1:
                await_taken(dve, key)
                dve.tensor_tensor(tiles(x, b), tiles(x, b), tiles(tm, b), ALU.add).then_inc(x_attended, 1)

        def dve_values(dve, a, b):
            key = ("v", a, b)
            ps = await_bank(dve, key).rearrange("p (t h d) -> p t h d", t=NT, d=DH)
            o = v_self[:, b % 2, :, :, 0:DH]
            if a == CAUSAL:
                bias = bcv("L0_xattn_b_qkv").rearrange("p (h d) -> p h d", d=DH).unsqueeze(1)
                dve.tensor_tensor(o, ps, bias.to_broadcast([P, NT, H, DH]), ALU.add).then_inc(frees(key), 1)
            else:
                dve.tensor_copy(o, ps).then_inc(frees(key), 1)

        def dve_mid(dve, key):
            o = op_no[key]
            m = B * S if key[0] == "kc" else T
            dve.wait_ge(rem_ready, o + 1)
            dve.tensor_copy(parts[:, o % 2, 1, 0:m], rem[:, o % 2, 0:m]).then_inc(mid_ready, 1)

        def dve_setup(dve):
            for buf in (v_self, vc_a, vc_b):
                dve.memset(buf[:], 1.0).then_inc(v_ones, 1)
            await_x(dve, "in", 0)
            dve_stats(dve, 0, 0, x)
            dve_hat(dve, 0, 0, x)
            dve.memset(words(q_stack[:, :]).bitcast(F32), 0.0).then_inc(q_zeroed, 1)

        def dve_context_values(dve, i):
            bias = bcv("L0_xattn_b_ckv")
            pair = await_bank(dve, ("vc", i))
            ps = pair[:, 0:T].rearrange("p (b h d) -> p b h d", b=B, d=DH)
            o = vc_a[:, i, :, :, 0:DH]
            if i == 0:
                bb = bias.rearrange("p (h d) -> p h d", d=DH).unsqueeze(1).to_broadcast([P, B, H, DH])
                dve.tensor_tensor(o, ps, bb, ALU.add)
            else:
                dve.tensor_copy(o, ps)
            ps = pair[:, T:2 * T].rearrange("p (b g j d) -> p b g j d", b=B, g=GROUPS, d=DH)
            for j in range(4):
                rr = slice(KB * j, KB * j + KB)
                o = vc_b[rr, i, :, :, 0:DH]
                if i == 0:
                    bb = bias[rr, :].rearrange("p (g j d) -> p g j d", g=GROUPS, d=DH)[:, :, j, :]
                    r = dve.tensor_tensor(o, ps[rr, :, :, j, :],
                                          bb.unsqueeze(1).to_broadcast([KB, B, GROUPS, DH]), ALU.add)
                else:
                    r = dve.tensor_copy(o, ps[rr, :, :, j, :])
            r.then_inc(frees(("vc", i)), 1)
            await_taken(dve, ("vc", i))
            for j in range(4):
                dve.memset(vc_b[KB * j:KB * j + KB - SB, i], 0.0).then_inc(once_only, 1)

        def dve_residual(dve, key, b, biased):
            ps = await_bank(dve, key).rearrange("p (t d) -> p t d", d=D)
            dve.wait_ge(x_biased[biased], b + 1)
            dve.tensor_tensor(tiles(x, b), ps, tiles(xb, b), ALU.add).then_inc(frees(key), 1)

        NORM_SRC = {0: (x, "in"), 1: (x, "att"), 2: (xb, "n2"), 3: (x, "b2"), 4: (x, "bo1"), 5: (x, "bo2"),
                    6: (tm, "pv"), 7: (tm, "m1"), 8: (tm, "pv"), 9: (tm, "c1"), 10: (tm, "h2")}
        G_D, B_D = "L2_xattn_g_d", "L2_xattn_b_d"
        AFFINE = {1: ("n2", xb, "L0_xattn_g2", "L0_xattn_be2"), 6: ("m1", tm, "L2_xattn_g_m", None),
                  7: ("m2", x, G_D, B_D), 8: ("c1", tm, "L2_xattn_g_c", None), 9: ("c2", x, G_D, B_D),
                  10: ("f", x, G_D, B_D)}

        def dve_stats_job(dve, k, b):
            src, what = NORM_SRC[k]
            if what == "pv":
                await_taken(dve, ("pv", "m" if k == 6 else "c", b))
            elif what in ("n2", "m1", "c1"):
                dve.wait_ge(affined[what], b + 1)
            elif what == "h2":
                dve.wait_ge(h2_ready, nth[("h2", b)])
                dve.tensor_tensor(tiles(tm, b), tiles(tm, b), tiles(x, b), ALU.add).then_inc(h2_added, 1)
                dve.wait_ge(h2_added, b + 1)
            else:
                await_x(dve, what, b)
            dve_stats(dve, k, b, src)

        def dve_job(dve, job):
            what, a, b = (*job, None)[0:3]
            if what == "out":
                dve_out(dve, a, b)
            elif what == "v":
                dve_values(dve, a, b)
            elif what == "mid":
                dve_mid(dve, job[1:])
            elif what == "vc":
                dve_context_values(dve, a)
            elif what == "stats":
                dve_stats_job(dve, a, b)
            elif what == "hat":
                dve_hat(dve, a, b, NORM_SRC[a][0])
            elif what == "ffn":
                dve_residual(dve, job, b, "b2" if a == CAUSAL else "bff2")
            elif what == "wo":
                dve_residual(dve, job, b, "bo1" if a == SELF else "bo2")
            elif what == "gate":
                for c in range(2):
                    ps = await_bank(dve, (*job, c))
                    for i in range(2):
                        m = 2 * c + i
                        dve.wait_ge(sig_ready, FC * (nth[job] - 1) + m + 1)
                        sig = tail[a][:, m * T:(m + 1) * T]
                        r = dve.scalar_tensor_tensor(out=sig, in0=ps[:, i * T:(i + 1) * T],
                                                     scalar=colv("L1_xattn_bff1", FC + m), in1=sig,
                                                     op0=ALU.add, op1=ALU.mult)
                    r.then_inc(frees((*job, c)), 1)
            elif what == "lin":
                await_slot(dve, ("ffn", CROSS, a))
                hid = slot(("ffn", CROSS, a))
                for c in range(2):
                    await_taken(dve, ("gate", a, c))
                    ps = await_bank(dve, (*job, c))
                    for i in range(2):
                        m = 2 * c + i
                        r = dve.scalar_tensor_tensor(out=hid[:, m, :], in0=ps[:, i * T:(i + 1) * T],
                                                     scalar=colv("L1_xattn_bff1", m),
                                                     in1=tail[a][:, m * T:(m + 1) * T],
                                                     op0=ALU.add, op1=ALU.mult)
                    r.then_inc(frees((*job, c)), 1)
            elif what == "vd":
                ps = await_bank(dve, job)
                dve.tensor_tensor(values_1("m", a, 0).rearrange("p (t d) -> p t d", d=D),
                                  ps.rearrange("p (t d) -> p t d", d=D), bct("L2_xattn_bv_m"), ALU.add)\
                   .then_inc(frees(job), 1)
            elif what == "vx":
                if a == "d":
                    await_bank(dve, ("Sd", "m", b, 1))
                ps = await_bank(dve, job)
                for kt, m in ((0, P), (1, SB)):
                    o, src = values_1(a, b, kt), ps[0:m, kt * D:(kt + 1) * D]
                    if a == "c":
                        r = dve.tensor_tensor(o, src, bcv("L2_xattn_bv_c")[0:m], ALU.add)
                    else:
                        r = dve.tensor_copy(o, src)
                r.then_inc(frees(job), 1)
            elif what == "Sd":
                for key, _, ts in sd_units(a, b):
                    ps = await_bank(dve, key).rearrange("p (i t) -> p i t", i=len(ts))
                    dve.tensor_reduce(nmx[:, b, ts[0]:ts[-1] + 1], ps[:, :, 0:KEYS[a]], AX.X, ALU.max,
                                      negate=True).then_inc(dmaxed, 1)
            elif what == "pv":
                for key, _, _ in sd_units(a, b):
                    await_taken(dve, key)
                dve.reciprocal(rinv[:, b, :], rsum[:, b, :]).then_inc(rinv_ready, 1)
                dve.wait_ge(rinv_ready, nth[job])
                ps = await_bank(dve, job)
                for t in range(NT):
                    i = NT * b + t
                    r = dve.scalar_tensor_tensor(out=tm[:, i, :], in0=ps[:, t * D:(t + 1) * D],
                                                 scalar=rinv[:, b, t:t + 1], in1=x[:, i, :],
                                                 op0=ALU.mult, op1=ALU.add)
                r.then_inc(frees(job), 1)
            elif what == "h2":
                ps = await_bank(dve, job).rearrange("p (t d) -> p t d", d=D)
                dve.tensor_tensor(tiles(tm, a), ps, bct("L2_xattn_f1_b"), ALU.add).then_inc(frees(job), 1)

        @block.vector
        def _(dve):
            dve_setup(dve)
            dve.wait_ge(consts, 7)
            dve.wait_ge(bc_loaded[0], 16 * BROADCAST_SETS[1])
            dve.wait_ge(v_ones, 3)
            for s in STEPS:
                if s["units"]:
                    dve_scores_max(dve, *s["units"])
                for job in s["jobs"]:
                    if job == ("hat", 1, 0):
                        dve.wait_ge(bc_loaded[1], 16 * (BROADCAST_SETS[2] - BROADCAST_SETS[1]))
                    dve_job(dve, job)

        def pool_rstd(pool, k, b):
            pool.wait_ge(moments[k], b + 1)
            pool.tensor_scalar(ve[:, b, :], mv[:, b, :, 1], EPS, None, ALU.add).then_inc(var_eps[k], 1)
            pool.wait_ge(var_eps[k], b + 1)
            pool.tensor_tensor(rs[:, b, :], ve[:, b, :], nhalf[:, :], ALU.pow).then_inc(rstd_ready[k], 1)

        BIASES = {"b2": ("att", "L0_xattn_b2"), "bo1": ("b2", "L1_xattn_bo1"), "bo2": ("bo1", "L1_xattn_bo2"),
                  "bff2": ("bo2", "L1_xattn_bff2"), "m": ("bff2", "L2_xattn_b_m"), "c": ("m", "L2_xattn_b_c")}

        def pool_bias(pool, key, b):
            after, name = BIASES[key]
            if (key, b) == ("b2", 0):
                pool.wait_ge(bc_loaded[1], 16 * (BROADCAST_SETS[2] - BROADCAST_SETS[1]))
            await_x(pool, after, b)
            if key == "b2":
                pool.wait_ge(hat_ready[2], b + 1)
            pool.tensor_tensor(tiles(xb, b), tiles(x, b), bct(name), ALU.add).then_inc(x_biased[key], 1)

        def pool_scaled_columns(pool):
            await_taken(pool, ("col", 1))
            for i, (src, m, f) in enumerate(((colv("L2_xattn_bq_m"), 1, 0.125), (colv("L2_xattn_bq_c"), 1, 0.125),
                                             (col[:, at_col["L1_xattn_bff1"] + FC:at_col["L1_xattn_bff1"] + 2 * FC],
                                              FC, 1.702))):
                pool.tensor_scalar(colx[:, 1 + i:1 + i + m], src, f, None, ALU.mult).then_inc(colx_ready, 1)

        def pool_rem(pool, key):
            o = op_no[key]
            m = B * S if key[0] == "kc" else T
            await_taken(pool, key)
            pool.tensor_tensor(rem[:, o % 2, 0:m], raw[:, o % 2, 0:m], parts[:, o % 2, 0, 0:m], ALU.subtract)\
                .then_inc(rem_ready, 1)

        def pool_low(pool, key):
            o = op_no[key]
            m = B * S if key[0] == "kc" else T
            pool.wait_ge(mid_ready, o + 1)
            pool.tensor_tensor(parts[:, o % 2, 2, 0:m], rem[:, o % 2, 0:m], parts[:, o % 2, 1, 0:m], ALU.subtract)\
                .then_inc(parts_ready, 1)

        def pool_minus_max(pool, a, n):
            c = NG * a + n
            if a == CAUSAL:
                pool.wait_ge(max_joined, n + 1)
            else:
                last = s_units(a)[-1]
                for j in (2, 3):
                    await_taken(pool, ("S", a, n, j, last[1], last[2]))
            m = (mxc if a == CROSS else mx)[:, c % 2, :, :]
            hi, lo, r = nm[:, c % 2, :, 0, :], nm[:, c % 2, :, 1, :], nmr[:, c % 2, :, :]
            pool.tensor_scalar(hi, m, -1.0, None, ALU.mult).then_inc(nm_step, 1)
            pool.wait_ge(nm_step, 2 * c + 1)
            pool.tensor_tensor(r, m, hi, ALU.add).then_inc(nm_step, 1)
            pool.wait_ge(nm_step, 2 * c + 2)
            pool.tensor_scalar(lo, r, -1.0, None, ALU.mult).then_inc(nm_ready, 1)

        @block.gpsimd
        def _(pool):
            pool.memset(ident[:, :], 0.0).then_inc(consts, 1)
            pool.memset(identb[:, :], 0.0).then_inc(consts, 1)
            pool.memset(mask[:, :], 0.0).then_inc(consts, 1)
            pool.wait_ge(consts, 3)
            for m in (ident, identb):
                pool.affine_select(out=m[:, :], in_=m[:, :], compare_op=ALU.not_equal, fill=1.0, base=0,
                                   pattern=[[-1, P]], channel_multiplier=1).then_inc(consts, 1)
            tri = mask[:, T - P:T]
            pool.affine_select(out=tri, in_=tri, compare_op=ALU.is_ge, fill=MASKED, base=0,
                               pattern=[[-1, P]], channel_multiplier=1).then_inc(consts, 1)
            pool.memset(nhalf[:, :], -0.5).then_inc(consts, 1)
            pool_rstd(pool, 0, 0)
            pool.wait_ge(rstd_ready[0], 1)
            for buf in (kc_stack, k_stack):
                pool.memset(buf[2 * KR:P].rearrange("p l a t -> p (l a t)").bitcast(F32), ONES).then_inc(ones_rows, 1)
            pool.wait_ge(ones_rows, 2)
            await_taken(pool, ("col", 0))
            pool.tensor_scalar(colx[:, 0:1], colv("L0_xattn_b_qkv"), HEAD_SCALE[CAUSAL], None, ALU.mult)\
                .then_inc(colx_ready, 1)
            pool.wait_ge(consts, 7)
            for s in STEPS:
                for job in s["jobs"]:
                    if job[0] == "nm":
                        pool_minus_max(pool, *job[1:])
                if s["step"] and s["step"][0:3] in mask_no and s["step"][3] == 1:
                    a, n, kt, _ = s["step"]
                    for half in range(2):
                        await_taken(pool, ("ST", a, n, kt, half))
                    e = slot((a, n, kt))[:, :, 0:P]
                    pool.affine_select(out=e, in_=e, compare_op=ALU.is_ge, fill=0.0, base=0,
                                       pattern=[[0, 4], [1, P]], channel_multiplier=-1)\
                        .then_inc(mask_done, 1)
                for job in s["jobs"]:
                    if job[0] in ("q", "k", "kc"):
                        pool_rem(pool, job)
                        if job == ("kc", 0):
                            pool_scaled_columns(pool)
                    elif job[0] == "mid":
                        pool_low(pool, job[1:])
                    elif job[0] == "stats":
                        pool_rstd(pool, *job[1:])
                    elif job[0] == "bias":
                        pool_bias(pool, *job[1:])

        def sp_parts_out(sp, key, dram, runs, m):
            o = op_no[key]
            sp.wait_ge(parts_ready, o + 1)
            for slot0, n, part, same in runs:
                src = parts[:, o % 2, part:part + (1 if same else n), 0:m]
                sp.dma_start(dram[:, slot0:slot0 + n, :], src.to_broadcast([P, n, m]) if same else src)\
                  .then_inc(bounced[o % 2], 16)

        def sp_stack_in(sp, o, dram, stack, done):
            sp.wait_ge(bounced[o % 2], BOUNCED * (o // 2 + 1))
            src = dram.rearrange("(pr par r) k t -> par (r k) pr t", par=2, r=DH)
            for par in range(2):
                sp.dma_start(stack(par), src[par]).then_inc(done, 16)

        def sp_keys_in(sp, a, b):
            kb = B * a + b
            if kb >= 2:
                await_bank(sp, ("acc", (kb - 2) // B, GROUPS * ((kb - 2) % B) + GROUPS - 1))
            sp_stack_in(sp, op_no[("k", a, b)], k_scratch[kb],
                        lambda par: k_stack[KR * par:KR * par + KR, kb % 2, :, :], k_stacked[kb % 2])

        def sp_queries_in(sp, c):
            a, n = divmod(c, NG)
            b, g = divmod(n, GROUPS)
            if c >= QR:
                a2, n2 = divmod(c - QR, NG)
                last = KEY_TILES[a2][-1]
                await_bank(sp, ("ST", a2, n2, last, 0 if last == "B" else 1))
            sp_stack_in(sp, op_no[("q", a, b)], q_scratch[B * a + b, 4 * g * DH:4 * (g + 1) * DH],
                        lambda par: q_stack[KR * par:KR * par + KR, c % QR, par::2, :], q_stacked[c % QR])

        def sp_round(sp, r):
            jobs = [job for s in STEPS if s["round"] == r for job in s["jobs"]]
            for what, a, n in [job for job in jobs if job[0] == "nm"]:
                c = NG * a + n
                await_taken(sp, ("nm", a, n))
                for k in range(2):
                    sp.dma_start(q_stack[NEG + k:NEG + k + 1, c % QR, :, :], nmt[4 * k:4 * k + 4, c % 2, :])\
                      .then_inc(neg_rows[c % 2], 16)
            split_now = [job[1:] for job in jobs if job[0] == "mid"]
            if r == -3:
                sp_parts_out(sp, ("q", CAUSAL, 0), q_scratch[0], Q_RUNS, T)
                sp_parts_out(sp, ("k", CAUSAL, 0), k_scratch[0], K_RUNS, T)
                sp_queries_in(sp, 0)
                sp_keys_in(sp, CAUSAL, 0)
                sp_context_stack(sp, 0)
                for c in range(1, 4):
                    sp_queries_in(sp, c)
                for name, _ in WEIGHTS[WEIGHT_SETS[1]:]:
                    load_weight(sp, name)
                for i in range(BROADCAST_SETS[1], BROADCAST_SETS[2]):
                    load_broadcast(sp, i)
                return
            for job in split_now:
                if job[0] == "kc":
                    sp_context_stack(sp, job[1])
                elif job[0] == "q":
                    sp_parts_out(sp, job, q_scratch[B * job[1] + job[2]], Q_RUNS, T)
                else:
                    sp_parts_out(sp, job, k_scratch[B * job[1] + job[2]], K_RUNS, T)
            if r > -2 and r + 5 < ROUNDS:
                sp_queries_in(sp, r + 5)
            for what, a, b in [job for job in split_now if job[0] == "k"]:
                sp_keys_in(sp, a, b)

        def sp_context_stack(sp, l):
            sp_parts_out(sp, ("kc", l), kc_scratch[l], K_RUNS, B * S)
            sp_stack_in(sp, op_no[("kc", l)], kc_scratch[l],
                        lambda par: kc_stack[KR * par:KR * par + KR, l, :, :], kc_stacked[l])

        def load_rows(sp, i0, i1):
            for name, n in COLUMNS[i0:i1]:
                i = int(i0 > 0)
                o = at_col[name] - i * FIRST_ROWS
                sp.dma_start(rows[i][o:o + n, :], inp[name][0:n * P].rearrange("(n p) -> n p", p=P))\
                  .then_inc(rows_loaded[i], 16)

        @block.sync
        def _(sp):
            sp.dma_start(tiles(x, 0), inp["x"][0].rearrange("(t p) d -> p t d", p=P)).then_inc(x_loaded[0], 16)
            load_rows(sp, 0, FIRST_COLUMNS)
            sp.dma_start(ctx_a[:, :, :], inp["ctx_1024"][:, 0:P, :].rearrange("b p d -> p b d"))\
              .then_inc(ctx_loaded, 16)
            sp.dma_start(ctx_b[:, :, :], inp["ctx_1024"][:, P:S, :].rearrange("b p d -> p b d"))\
              .then_inc(ctx_loaded, 16)
            load_rows(sp, FIRST_COLUMNS, len(COLUMNS))
            for b in range(1, B):
                sp.dma_start(tiles(x, b), inp["x"][b].rearrange("(t p) d -> p t d", p=P)).then_inc(x_loaded[b], 16)
            sp.wait_ge(ones_rows, 2)
            sp.wait_ge(q_zeroed, 1)
            for r in range(-3, ROUNDS + 2):
                sp_round(sp, r)
            for b in range(B):
                await_taken(sp, ("pv", "d", b))
                sp.dma_start(out[b].rearrange("(t p) d -> p t d", p=P), tiles(tm, b)).then_inc(stored, 16)
            sp.wait_ge(stored, 16 * B)


def kernel(**inputs):
    import numpy as np
    import concourse.bacc as bacc
    from concourse.bass_utils import run_bass_kernel_spmd

    nc = bacc.Bacc("TRN2", target_bir_lowering=False, num_devices=1)
    arrays, aps = {}, {}
    for name, value in inputs.items():
        a = np.ascontiguousarray(value)
        arrays[f"in_{name}"] = a
        aps[name] = nc.dram_tensor(f"in_{name}", a.shape, mybir.dt.from_np(a.dtype), kind="ExternalInput").ap()
    out = nc.dram_tensor("out_x", (B, T, D), F32, kind="ExternalOutput").ap()
    four_cross_attention_blocks(nc, out, **aps)
    got = run_bass_kernel_spmd(nc, [arrays], core_ids=[0])
    return got.results[0]["out_x"]
```
